# Optimizing a Trainium2 kernel written in Bass

```python
import numpy as np
import jax
import jax.numpy as jnp

def _softmax(x, axis=-1):
    return jax.nn.softmax(x, axis=axis)
def _gelu(x):
    return jax.nn.gelu(x, approximate=True)
def _silu(x):
    return jax.nn.silu(x)
def _sigmoid(x):
    return jax.nn.sigmoid(x)
def _layernorm(x, axis=-1, eps=1e-5):
    m = jnp.mean(x, axis=axis, keepdims=True)
    v = jnp.var(x, axis=axis, keepdims=True)
    return (x - m) / jnp.sqrt(v + eps)
def _scatter_add(tgt, idx, src, axis=0):
    return tgt.at[idx].add(src)
def _segment_sum(src, seg, n):
    return jax.ops.segment_sum(src, seg, n)

kernel_name = 'mk_conv_seq_d1_conv_nchw512_e7c5f2'

def setup_inputs(seed: int = 0):
    np.random.seed(seed)
    _w = jnp.asarray
    def _rec_inputs():
        import jax
        import jax.numpy as jnp
        _gk = jax.random.key(seed)
        x = 7.22e-05 + 1 * jax.random.normal(jax.random.fold_in(_gk, 1), (16, 512, 32, 32), jnp.float32)
        return x
    x = _rec_inputs()
    def _L0_conv_setup():
        import jax, jax.numpy as jnp
        import numpy as np
        B, C, H, W = (16, 512, 32, 32)
        NUM_HEADS = 4
        HEAD_SIZE = C // NUM_HEADS
        EPS = 1e-05

        def _attention_block(x, gn_weight, gn_bias, qkv_w, qkv_b, out_w, out_b):
            b, c, h, w = x.shape
            mean = jnp.mean(x, axis=(1, 2, 3), keepdims=True)
            var = jnp.var(x, axis=(1, 2, 3), keepdims=True)
            y = (x - mean) / jnp.sqrt(var + EPS)
            y = y * gn_weight[None, :, None, None] + gn_bias[None, :, None, None]
            s = h * w
            y = y.reshape(b, c, s).transpose(0, 2, 1)
            qkv = y @ qkv_w.T + qkv_b
            q, k, v = jnp.split(qkv, 3, axis=-1)

            def heads(t):
                return t.reshape(b, s, NUM_HEADS, HEAD_SIZE).transpose(0, 2, 1, 3)
            q, k, v = (heads(q), heads(k), heads(v))
            scale = 1.0 / jnp.sqrt(jnp.float32(HEAD_SIZE))
            attn = jnp.einsum('bhqd,bhkd->bhqk', q, k) * scale
            attn = jax.nn.softmax(attn, axis=-1)
            o = jnp.einsum('bhqk,bhkd->bhqd', attn, v)
            o = o.transpose(0, 2, 1, 3).reshape(b, s, c)
            o = o @ out_w.T + out_b
            o = o.transpose(0, 2, 1).reshape(b, c, h, w)
            return x + o
        key = jax.random.key(seed)
        k1, k2, k3 = jax.random.split(key, 3)
        x = jax.random.normal(k1, (B, C, H, W), dtype=jnp.float32)
        qkv_w = jax.random.normal(k2, (3 * C, C), dtype=jnp.float32) * (1.0 / np.sqrt(C))
        qkv_b = jnp.zeros((3 * C,), dtype=jnp.float32)
        out_w = jax.random.normal(k3, (C, C), dtype=jnp.float32) * (1.0 / np.sqrt(C))
        out_b = jnp.zeros((C,), dtype=jnp.float32)
        gn_weight = jnp.ones((C,), dtype=jnp.float32)
        gn_bias = jnp.zeros((C,), dtype=jnp.float32)
        return {'x': x, 'gn_weight': gn_weight, 'gn_bias': gn_bias, 'qkv_w': qkv_w, 'qkv_b': qkv_b, 'out_w': out_w, 'out_b': out_b}
    _L0_conv_all = _L0_conv_setup()
    _L0_conv_in = {k: v for k, v in _L0_conv_all.items() if k in ('gn_weight', 'gn_bias', 'qkv_w', 'qkv_b', 'out_w', 'out_b', )}
    del _L0_conv_all

    return {
        "x": x,
        "L0_conv_gn_weight": _L0_conv_in["gn_weight"],
        "L0_conv_gn_bias": _L0_conv_in["gn_bias"],
        "L0_conv_qkv_w": _L0_conv_in["qkv_w"],
        "L0_conv_qkv_b": _L0_conv_in["qkv_b"],
        "L0_conv_out_w": _L0_conv_in["out_w"],
        "L0_conv_out_b": _L0_conv_in["out_b"],
    }

def reference(x, L0_conv_gn_weight, L0_conv_gn_bias, L0_conv_qkv_w, L0_conv_qkv_b, L0_conv_out_w, L0_conv_out_b):
    import jax
    import jax.numpy as jnp
    def _L0_conv_ref(x, gn_weight, gn_bias, qkv_w, qkv_b, out_w, out_b):
        import jax, jax.numpy as jnp
        import numpy as np
        B, C, H, W = (16, 512, 32, 32)
        NUM_HEADS = 4
        HEAD_SIZE = C // NUM_HEADS
        EPS = 1e-05

        def _attention_block(x, gn_weight, gn_bias, qkv_w, qkv_b, out_w, out_b):
            b, c, h, w = x.shape
            mean = jnp.mean(x, axis=(1, 2, 3), keepdims=True)
            var = jnp.var(x, axis=(1, 2, 3), keepdims=True)
            y = (x - mean) / jnp.sqrt(var + EPS)
            y = y * gn_weight[None, :, None, None] + gn_bias[None, :, None, None]
            s = h * w
            y = y.reshape(b, c, s).transpose(0, 2, 1)
            qkv = y @ qkv_w.T + qkv_b
            q, k, v = jnp.split(qkv, 3, axis=-1)

            def heads(t):
                return t.reshape(b, s, NUM_HEADS, HEAD_SIZE).transpose(0, 2, 1, 3)
            q, k, v = (heads(q), heads(k), heads(v))
            scale = 1.0 / jnp.sqrt(jnp.float32(HEAD_SIZE))
            attn = jnp.einsum('bhqd,bhkd->bhqk', q, k) * scale
            attn = jax.nn.softmax(attn, axis=-1)
            o = jnp.einsum('bhqk,bhkd->bhqd', attn, v)
            o = o.transpose(0, 2, 1, 3).reshape(b, s, c)
            o = o @ out_w.T + out_b
            o = o.transpose(0, 2, 1).reshape(b, c, h, w)
            return x + o
        return _attention_block(x, gn_weight, gn_bias, qkv_w, qkv_b, out_w, out_b)

    def _gn(v, G=32, eps=1e-5):
        B_, C_, H_, W_ = v.shape
        g = v.reshape(B_, G, C_ // G, H_, W_)
        m = jnp.mean(g, axis=(2, 3, 4), keepdims=True)
        s = jnp.var(g, axis=(2, 3, 4), keepdims=True)
        return ((g - m) / jnp.sqrt(s + eps)).reshape(v.shape)

    def _ln_c(v, eps=1e-6):
        m = jnp.mean(v, axis=1, keepdims=True)
        s = jnp.var(v, axis=1, keepdims=True)
        return (v - m) / jnp.sqrt(s + eps)

    def _ln_t(v, eps=1e-5):
        m = jnp.mean(v, axis=-1, keepdims=True)
        s = jnp.var(v, axis=-1, keepdims=True)
        return (v - m) / jnp.sqrt(s + eps)

    def _to_tokens(v):
        B_, C_, H_, W_ = v.shape
        return v.reshape(B_, C_, H_ * W_).transpose(0, 2, 1)
    def _from_tokens(t, like):
        B_, C_, H_, W_ = like.shape
        return t.transpose(0, 2, 1).reshape(B_, C_, H_, W_)

    x = _L0_conv_ref(x, L0_conv_gn_weight, L0_conv_gn_bias, L0_conv_qkv_w, L0_conv_qkv_b, L0_conv_out_w, L0_conv_out_b)
    return x


_drawn_inputs = setup_inputs


def setup_inputs(seed=0):
    import zlib

    import numpy as np

    out = dict(_drawn_inputs(seed))
    spreads = {'L0_conv_gn_weight': (1.0, 0.2),
     'L0_conv_gn_bias': (0.0, 0.1),
     'L0_conv_qkv_b': (0.0, 0.1),
     'L0_conv_out_b': (0.0, 0.1)}
    factors = {}
    for name, (base, spread) in spreads.items():
        noise = np.random.default_rng([zlib.crc32(name.encode()), seed]).standard_normal(out[name].shape)
        drawn = base * np.exp(spread * noise) if base else spread * noise
        out[name] = jnp.asarray(drawn.astype(out[name].dtype))
    for name, factor in factors.items():
        out[name] = (out[name] * factor).astype(out[name].dtype)
    return out
```

```python
from contextlib import ExitStack

import concourse.bass as bass
from concourse import mybir

F32 = mybir.dt.float32
F32R = mybir.dt.float32r
ALU = mybir.AluOpType
ACT = mybir.ActivationFunctionType
AX_X = mybir.AxisListType.X

P = 128
BATCHES, C, S = 16, 512, 1024
HEADS = 4
D = C // HEADS
CC = C // P
KEYS = S // P
HALF = 512
TILES = HALF // P
UNITS = 2 * HEADS
EPS = 1e-5
Q, K, V = 0, 1, 2
RING = 3
BN = 6

GAMMA, BETA, QKV_B, OUT_B = 0, CC, 2 * CC, 2 * CC + 3 * HEADS
VECTORS = OUT_B + CC


def fills(u, last):
    h, half = divmod(u, 2)
    if half == 0:
        after = [("turn_v", h, 1)]
        if u == 4 and not last:
            after.append(("mean", 0, 0))
        return [("turn_v", h, 0), ("vt", h, 1)], ("q", h, 1), after
    if h < HEADS - 1:
        after = [("variance", 0, 0)] if u == 5 and not last else []
        return [("vt", h + 1, 0), ("k", h + 1, 0)], ("q", h + 1, 0), after
    project = [("project", 0, m) for m in range(CC)]
    if last:
        return project[:-1], project[-1], []
    return project + [("vt", 0, 0), ("k", 0, 0)], ("q", 0, 0), []


def in_ring(step):
    kind, _, n = step
    return kind in ("vt", "turned") or (kind, n) in (("turn_v", 0), ("project", 0))


def split_in_two(step):
    return step[0] in ("q", "k", "turn_v", "turned")


def score_banks(step):
    kind, h, n = step
    if kind == "k":
        return 0, 1
    if kind == "q":
        return (0,) if n == 1 else (3,) if h == 0 else (2,)
    return {"turn_v": (1,), "mean": (2,), "variance": (3,), "project": (n - 1,)}[kind]


class Tally:

    def __init__(self):
        self.ring = self.ring_hi = self.bank = self.bank_hi = 0

    def add(self, step):
        if in_ring(step):
            self.ring += 1
            self.ring_hi += split_in_two(step)
        else:
            self.bank += 1
            self.bank_hi += split_in_two(step)


def results(u, last):
    before, slipped, after = fills(u, last)
    return (before + [("turned", 0, 0), ("turned", 0, 1), slipped] + after
            + [("turned", 0, c) for c in range(2, KEYS)])


TAIL = [("project", 1, m) for m in range(CC)]
HEAD_START = [("mean", 0, 0), ("variance", 0, 0), ("vt", 0, 0), ("k", 0, 0), ("q", 0, 0)]
START, BATCH = Tally(), Tally()
for _step in HEAD_START:
    START.add(_step)
for _u in range(UNITS):
    for _step in results(_u, False):
        BATCH.add(_step)
for _step in TAIL:
    BATCH.add(_step)
assert BATCH.ring % RING == 0


def attention_program(nc, x, w_qkv, w_out, vectors, out):
    ctx = ExitStack()
    with ctx:
        def sb(name, shape, dt=F32):
            return ctx.enter_context(nc.sbuf_tensor(name, shape, dt))

        def ps(name, shape):
            return ctx.enter_context(nc.psum_tensor(name, shape, F32))

        def sem(name):
            return ctx.enter_context(nc.semaphore(name))

        w_hi = sb("w_hi", [P, HEADS, 3, CC, D], F32R)
        w_lo = sb("w_lo", [P, HEADS, 3, CC, D], F32R)
        wo_hi = sb("wo_hi", [P, HEADS, C], F32R)
        wo_lo = sb("wo_lo", [P, HEADS, C], F32R)
        x_in = sb("x_in", [P, CC, S])
        y_hi = sb("y_hi", [P, CC, S], F32R)
        y_lo = sb("y_lo", [P, CC, S], F32R)
        q_hi = sb("q_hi", [P, HALF], F32R)
        q_lo = sb("q_lo", [P, HALF], F32R)
        k_hi = sb("k_hi", [P, S], F32R)
        k_lo = sb("k_lo", [P, S], F32R)
        vt = sb("vt", [P, S])
        v_hi = sb("v_hi", [P, KEYS, D], F32R)
        v_lo = sb("v_lo", [P, KEYS, D], F32R)
        probs = sb("probs", [P, TILES, S])
        turned_hi = sb("turned_hi", [P, RING, HALF], F32R)
        turned_lo = sb("turned_lo", [P, RING, HALF], F32R)
        o_hi = sb("o_hi", [P, HEADS, S], F32R)
        o_lo = sb("o_lo", [P, HEADS, S], F32R)
        rows = sb("rows", [P, CC, HALF])
        vec = sb("vec", [P, VECTORS])
        ident = sb("ident", [P, P])
        average = sb("average", [P, P])
        minus_half = sb("minus_half", [P, 1])
        bn = sb("bn", [P, 2 * CC, BN])
        part = sb("part", [P, 2])
        neg_mean = sb("neg_mean", [P, 1])
        offset = sb("offset", [P, 1])
        spread = sb("spread", [P, 1])
        variance = sb("variance", [P, 1])
        rstd = sb("rstd", [P, 1])
        gain = sb("gain", [P, CC])
        neg_max = sb("neg_max", [P, TILES])
        row_sum = sb("row_sum", [P, TILES])
        row_scale = sb("row_scale", [P, TILES])

        bank = ps("bank", [P, 4, HALF])
        ring = ps("ring", [P, RING, HALF])
        attended = ps("attended", [P, HALF])

        stage = probs[:, :, :].rearrange("p (s t) n -> p s (t n)", s=2)

        vec_loaded = sem("vec_loaded")
        stage_loaded = [sem(f"stage_loaded{i}") for i in range(2)]
        x_loaded = [sem(f"x_loaded{i}") for i in range(CC)]
        rows_loaded = [sem(f"rows_loaded{i}") for i in range(CC)]
        rows_stored = [sem(f"rows_stored{i}") for i in range(CC)]
        constants_set = sem("constants_set")
        ident_cleared = sem("ident_cleared")
        q_bias_scaled = sem("q_bias_scaled")
        weight_hi = sem("weight_hi")
        weight_split = sem("weight_split")
        bn_done = sem("bn_done")
        part_ready = sem("part_ready")
        offset_ready = sem("offset_ready")
        spread_ready = sem("spread_ready")
        rstd_ready = sem("rstd_ready")
        gain_ready = sem("gain_ready")
        normalised = sem("normalised")
        y_hi_ready = sem("y_hi_ready")
        y_ready = sem("y_ready")
        scores_ready = sem("scores_ready")
        max_ready = sem("max_ready")
        exp_ready = sem("exp_ready")
        scale_ready = sem("scale_ready")
        probs_ready = sem("probs_ready")
        ring_ready = sem("ring_ready")
        ring_hi = sem("ring_hi")
        ring_free = sem("ring_free")
        bank_ready = sem("bank_ready")
        bank_hi = sem("bank_hi")
        bank_free = sem("bank_free")
        attend_done = sem("attend_done")
        o_hi_ready = sem("o_hi_ready")
        attended_free = sem("attended_free")
        rows_ready = sem("rows_ready")
        dve_turn = sem("dve_turn")
        pool_turn = sem("pool_turn")

        pieces = [(w_hi[:, h, :, :, :].rearrange("p a c d -> p (a c d)"),
                   w_lo[:, h, :, :, :].rearrange("p a c d -> p (a c d)")) for h in range(HEADS)]
        pieces.append((wo_hi[:, :, :].rearrange("p h n -> p (h n)"),
                       wo_lo[:, :, :].rearrange("p h n -> p (h n)")))
        QUERY = CC * D
        SCALE = float(D) ** -0.5

        def parts(i):
            n = HEADS * C if i == HEADS else 3 * QUERY
            return [(0, n, 1.0)] if i == HEADS else [(0, QUERY, SCALE), (QUERY, n, 1.0)]

        def bias(step):
            kind, h, n = step
            at = {"q": QKV_B + Q * HEADS + h, "k": QKV_B + K * HEADS + h,
                  "vt": QKV_B + V * HEADS + h, "project": OUT_B + n}[kind]
            return vec[:, at:at + 1]

        def psum_of(step, n):
            if in_ring(step):
                return ring[:, n.ring % RING, :]
            banks = score_banks(step)
            if len(banks) == 2:
                return bank[:, 0:2, :].rearrange("p b n -> p (b n)")
            return bank[:, banks[0], :]

        def pair_of(step):
            kind, h, n = step
            if kind == "q":
                return q_hi[:, :], q_lo[:, :]
            if kind == "k":
                return k_hi[:, :], k_lo[:, :]
            if kind == "turn_v":
                a = n * KEYS // 2
                return tuple(v[:, a:a + KEYS // 2, :].rearrange("p c d -> p (c d)") for v in (v_hi, v_lo))
            return turned_hi[:, n % RING, :], turned_lo[:, n % RING, :]

        def x_of(b, m, half):
            return x[b, m * P:(m + 1) * P, half * HALF:(half + 1) * HALF]

        block = ctx.enter_context(nc.Block())

        @block.sync
        def _(sp):
            for c in range(CC):
                sp.dma_start(x_in[:, c, :], x[0, c * P:(c + 1) * P, :]).then_inc(x_loaded[c], 16)
            for i in range(2, HEADS + 1):
                sp.wait_ge(weight_split, i - 1)
                n = parts(i)[-1][1]
                src = w_out if i == HEADS else w_qkv[:, i, :]
                sp.dma_start(stage[:, i % 2, 0:n], src).then_inc(stage_loaded[i % 2], 16)
            for m in range(CC):
                sp.dma_start(rows[:, m, :], x_of(0, m, 0)).then_inc(rows_loaded[m], 16)

            def batch(b, last):
                if not last:
                    sp.wait_ge(y_ready, b + 1)
                    for c in range(CC):
                        sp.dma_start(x_in[:, c, :], x[b + 1, c * P:(c + 1) * P, :]).then_inc(x_loaded[c], 16)
                for half in range(2):
                    for m in range(CC):
                        sp.wait_ge(rows_ready, 2 * CC * b + CC * half + m + 1)
                        sp.dma_start(out[b, m * P:(m + 1) * P, half * HALF:(half + 1) * HALF],
                                     rows[:, m, :]).then_inc(rows_stored[m], 16)
                    if half == 1 and last:
                        continue
                    for m in range(CC):
                        sp.wait_ge(rows_stored[m], 32 * b + 16 * half + 16)
                        sp.dma_start(rows[:, m, :], x_of(b + half, m, 1 - half)).then_inc(rows_loaded[m], 16)

            with sp.Fori(0, BATCHES - 1) as b:
                batch(b, False)
            batch(BATCHES - 1, True)
            for m in range(CC):
                sp.wait_ge(rows_stored[m], 32 * BATCHES)

        @block.gpsimd
        def _(pool):
            pool.memset(ident[:, :], 0.0).then_inc(ident_cleared, 1)
            pool.memset(average[:, :], 1.0 / P).then_inc(constants_set, 1)
            pool.memset(minus_half[:, :], -0.5).then_inc(constants_set, 1)
            pool.wait_ge(ident_cleared, 1)
            pool.affine_select(out=ident[:, :], in_=ident[:, :], compare_op=ALU.not_equal, fill=1.0, base=0,
                               pattern=[[-1, P]], channel_multiplier=1).then_inc(constants_set, 1)

            def hold(semaphore, value):
                pool.wait_ge(semaphore, value)
                pool.sem_inc(pool_turn, 1)

            def normalise(b, variance_at):
                pool.wait_ge(bank_free, variance_at)
                pool.tensor_tensor(rstd[:, :], variance[:, :], minus_half[:, :], ALU.pow).then_inc(rstd_ready, 1)
                pool.wait_ge(rstd_ready, b + 1)
                pool.tensor_tensor(gain[:, :], vec[:, GAMMA:GAMMA + CC], rstd[:, 0:1].broadcast_to([P, CC]),
                                   ALU.mult).then_inc(gain_ready, 1)
                hold(gain_ready, b + 1)
                for c in range(CC):
                    pool.tensor_scalar(x_in[:, c, :], x_in[:, c, :], neg_mean[:, 0:1], gain[:, c:c + 1],
                                       ALU.add, ALU.mult).then_inc(normalised, 1)

            def scale_rows(unit):
                for t in range(TILES):
                    hold(scale_ready, TILES * unit + t + 1)
                    pool.tensor_scalar(probs[:, t, :], probs[:, t, :], row_scale[:, t:t + 1], 1.0,
                                       ALU.mult, ALU.mult).then_inc(probs_ready, 1)

            pool.wait_ge(constants_set, 3)
            pool.wait_ge(vec_loaded, 16)
            normalise(0, 2)
            scale_rows(0)

            def batch(b, last):
                n = Tally()
                for u in range(UNITS):
                    for step in results(u, last):
                        n.add(step)
                        if step[0] == "variance":
                            variance_at = START.bank + BATCH.bank * b + n.bank
                    if u == 5 and not last:
                        normalise(b + 1, variance_at)
                    if u < UNITS - 1 or not last:
                        scale_rows(UNITS * b + u + 1)

            with pool.Fori(0, BATCHES - 1) as b:
                batch(b, False)
            batch(BATCHES - 1, True)

        @block.scalar
        def _(act):
            act.dma_start(vec[:, :], vectors).then_inc(vec_loaded, 16)
            for i in range(2):
                act.dma_start(stage[:, i, 0:3 * QUERY], w_qkv[:, i, :]).then_inc(stage_loaded[i], 16)

            def weights(i):
                act.wait_ge(stage_loaded[i % 2], 16 * (i // 2 + 1))
                for a, z, factor in parts(i):
                    act.activation(pieces[i][0][:, a:z], stage[:, i % 2, a:z], ACT.Copy,
                                   scale=factor).then_inc(weight_hi, 1)

            def y_parts(b):
                for c in range(CC):
                    act.wait_ge(normalised, CC * b + c + 1)
                    act.activation(y_hi[:, c, :], x_in[:, c, :], ACT.Identity,
                                   bias=vec[:, BETA + c:BETA + c + 1]).then_inc(y_hi_ready, 1)

            def hi_part(step, b, n):
                if in_ring(step):
                    act.wait_ge(ring_ready, START.ring + BATCH.ring * b + n.ring + 1)
                    done = ring_hi
                else:
                    act.wait_ge(bank_ready, START.bank + BATCH.bank * b + n.bank + 1)
                    done = bank_hi
                if step[0] in ("q", "k"):
                    act.activation(pair_of(step)[0], psum(step, n), ACT.Identity, bias=bias(step)).then_inc(done, 1)
                else:
                    act.activation(pair_of(step)[0], psum(step, n), ACT.Copy).then_inc(done, 1)

            def psum(step, n):
                n.ring += START.ring
                where = psum_of(step, n)
                n.ring -= START.ring
                return where

            def exponentials(unit, turned=None):
                for t in range(TILES):
                    if turned is not None and t == 0:
                        act.wait_ge(ring_ready, turned)
                    act.wait_ge(max_ready, TILES * unit + t + 1)
                    s = 2 * (t % 2)
                    act.activation(probs[:, t, :], bank[:, s:s + 2, :].rearrange("p b n -> p (b n)"), ACT.Exp,
                                   bias=neg_max[:, t:t + 1], accum_out=row_sum[:, t:t + 1]).then_inc(exp_ready, 1)

            weights(0)
            y_parts(0)
            for i in range(1, HEADS + 1):
                weights(i)
            act.wait_ge(q_bias_scaled, 1)
            before = Tally()
            for step in HEAD_START:
                if split_in_two(step):
                    act.wait_ge(bank_ready, before.bank + 1)
                    act.activation(pair_of(step)[0], psum_of(step, before), ACT.Identity,
                                   bias=bias(step)).then_inc(bank_hi, 1)
                before.add(step)
            act.wait_ge(weight_split, HEADS + 1)
            exponentials(0)

            def batch(b, last):
                n = Tally()
                for u in range(UNITS):
                    h, half = divmod(u, 2)
                    if u == UNITS - 1 and not last:
                        y_parts(b + 1)
                    for step in results(u, last):
                        if step[0] == "turned" and step[2] >= RING:
                            act.wait_ge(attend_done, KEYS * (UNITS * b + u) + step[2] - RING + 1)
                        if split_in_two(step):
                            hi_part(step, b, n)
                        n.add(step)
                    act.wait_ge(attend_done, KEYS * (UNITS * b + u + 1))
                    act.activation(o_hi[:, h, half * HALF:(half + 1) * HALF], attended[:, :],
                                   ACT.Copy).then_inc(o_hi_ready, 1)
                    if u < UNITS - 1 or not last:
                        exponentials(UNITS * b + u + 1, START.ring + BATCH.ring * b + n.ring)

            with act.Fori(0, BATCHES - 1) as b:
                batch(b, False)
            batch(BATCHES - 1, True)

        @block.vector
        def _(dve):
            def weights(i):
                for n, (a, z, factor) in enumerate(parts(i)):
                    dve.wait_ge(weight_hi, 2 * i + n + 1)
                    lo = dve.scalar_tensor_tensor(pieces[i][1][:, a:z], stage[:, i % 2, a:z], factor,
                                                  pieces[i][0][:, a:z].bitcast(F32), ALU.mult, ALU.subtract)
                lo.then_inc(weight_split, 1)

            def partition_statistics(b):
                for c in range(CC):
                    dve.wait_ge(x_loaded[c], 16 * b + 16)
                    for half in range(2):
                        dve.bn_stats(bn[:, 2 * c + half, :],
                                     x_in[:, c, half * HALF:(half + 1) * HALF]).then_inc(bn_done, 1)
                dve.wait_ge(bn_done, 2 * CC * (b + 1))
                dve.sem_inc(dve_turn, 1)
                dve.bn_aggr(part[:, :], bn[:, :, :].rearrange("p a s -> p (a s)")).then_inc(part_ready, 1)

            def whole_mean(b, psum, ready_at):
                dve.wait_ge(bank_ready, ready_at)
                dve.tensor_scalar(neg_mean[:, :], psum[:, 0:1], -1.0, None, ALU.mult).then_inc(bank_free, 1)
                dve.wait_ge(bank_free, ready_at)
                dve.tensor_tensor(offset[:, :], part[:, 0:1], neg_mean[:, :], ALU.add).then_inc(offset_ready, 1)
                dve.wait_ge(offset_ready, b + 1)
                dve.scalar_tensor_tensor(spread[:, :], offset[:, :], offset[:, 0:1], part[:, 1:2], ALU.mult,
                                         ALU.add).then_inc(spread_ready, 1)

            def whole_variance(psum, ready_at):
                dve.wait_ge(bank_ready, ready_at)
                dve.tensor_scalar(variance[:, :], psum[:, 0:1], EPS, None, ALU.add).then_inc(bank_free, 1)

            def y_parts(b):
                for c in range(CC):
                    dve.wait_ge(y_hi_ready, CC * b + c + 1)
                    lo = dve.scalar_tensor_tensor(y_lo[:, c, :], x_in[:, c, :], vec[:, BETA + c:BETA + c + 1],
                                                  y_hi[:, c, :].bitcast(F32), ALU.add, ALU.subtract)
                lo.then_inc(y_ready, 1)

            def softmax(unit):
                def maximum(t):
                    dve.wait_ge(scores_ready, TILES * unit + t + 1)
                    s = 2 * (t % 2)
                    dve.tensor_reduce(neg_max[:, t:t + 1], bank[:, s:s + 2, :].rearrange("p b n -> p (b n)"),
                                      AX_X, ALU.max, negate=True).then_inc(max_ready, 1)

                def inverse(t):
                    dve.wait_ge(exp_ready, TILES * unit + t + 1)
                    dve.reciprocal(row_scale[:, t:t + 1], row_sum[:, t:t + 1]).then_inc(scale_ready, 1)

                maximum(0)
                for t in range(1, TILES):
                    maximum(t)
                    if t > 1:
                        inverse(t - 2)
                inverse(TILES - 2)
                inverse(TILES - 1)

            def finish(step, b, n, start=START):
                kind, h, m = step
                ring_at = start.ring + BATCH.ring * b + n.ring + 1
                bank_at = start.bank + BATCH.bank * b + n.bank + 1
                at_start = Tally()
                at_start.ring = start.ring + n.ring
                psum = psum_of(step, at_start)
                free = ring_free if in_ring(step) else bank_free
                if kind == "mean":
                    whole_mean(b + (start is START), psum, bank_at)
                elif kind == "variance":
                    whole_variance(psum, bank_at)
                elif split_in_two(step):
                    hi, lo = pair_of(step)
                    if in_ring(step):
                        dve.wait_ge(ring_hi, BATCH.ring_hi * b + n.ring_hi + 1)
                    else:
                        dve.wait_ge(bank_hi, start.bank_hi + BATCH.bank_hi * b + n.bank_hi + 1)
                    if kind in ("q", "k"):
                        dve.scalar_tensor_tensor(lo, psum, bias(step), hi.bitcast(F32), ALU.add,
                                                 ALU.subtract).then_inc(free, 1)
                    else:
                        dve.tensor_tensor(lo, psum, hi.bitcast(F32), ALU.subtract).then_inc(free, 1)
                elif kind == "vt":
                    dve.wait_ge(ring_ready, ring_at)
                    dve.tensor_scalar(vt[:, m * HALF:(m + 1) * HALF], psum, bias(step), None,
                                      ALU.add).then_inc(free, 1)
                else:
                    if in_ring(step):
                        dve.wait_ge(ring_ready, ring_at)
                    else:
                        dve.wait_ge(bank_ready, bank_at)
                    dve.wait_ge(rows_loaded[m], 32 * b + 16 * h + 16)
                    dve.scalar_tensor_tensor(rows[:, m, :], psum, bias(step), rows[:, m, :], ALU.add,
                                             ALU.add).then_inc(rows_ready, 1)
                    dve.wait_ge(rows_ready, 2 * CC * b + CC * h + m + 1)
                    dve.sem_inc(free, 1)

            dve.wait_ge(vec_loaded, 16)
            dve.tensor_scalar(vec[:, QKV_B:QKV_B + HEADS], vec[:, QKV_B:QKV_B + HEADS], SCALE, None,
                              ALU.mult).then_inc(q_bias_scaled, 1)
            dve.memset(offset[:, :], 0.0).then_inc(attended_free, 1)
            partition_statistics(0)
            before = Tally()
            for step in HEAD_START[:2]:
                finish(step, 0, before, Tally())
                before.add(step)
            weights(0)
            y_parts(0)
            for i in range(1, HEADS + 1):
                weights(i)
            for step in HEAD_START[2:]:
                finish(step, 0, before, Tally())
                before.add(step)
            softmax(0)

            def batch(b, last):
                n = Tally()
                for u in range(UNITS):
                    h, half = divmod(u, 2)
                    if u == 3 and not last:
                        partition_statistics(b + 1)
                    if u == UNITS - 1 and not last:
                        y_parts(b + 1)
                    for step in results(u, last):
                        finish(step, b, n)
                        n.add(step)
                    dve.wait_ge(o_hi_ready, UNITS * b + u + 1)
                    at = slice(half * HALF, (half + 1) * HALF)
                    dve.tensor_tensor(o_lo[:, h, at], attended[:, :], o_hi[:, h, at].bitcast(F32),
                                      ALU.subtract).then_inc(attended_free, 1)
                    if u < UNITS - 1 or not last:
                        softmax(UNITS * b + u + 1)
                for step in TAIL:
                    finish(step, b, n)
                    n.add(step)

            with dve.Fori(0, BATCHES - 1) as b:
                batch(b, False)
            batch(BATCHES - 1, True)

        @block.tensor
        def _(pe):
            def product(psum, a, z, stationary, moving, contractions, begin=0, end=None):
                end = contractions if end is None else end
                for i in range(begin, end):
                    s_hi, s_lo = stationary(i)
                    m_hi, m_lo = moving(i)
                    nc.tensor.matmul(psum[:, a:z], s_hi, m_hi, start=(i == 0), stop=False)
                    nc.tensor.matmul(psum[:, a:z], s_hi, m_lo, start=False, stop=False)
                    done = nc.tensor.matmul(psum[:, a:z], s_lo, m_hi, start=False, stop=(i == contractions - 1))
                return done

            def project_y(psum, h, which, half, begin=0, end=None):
                at = slice(half * HALF, (half + 1) * HALF)
                return product(psum, 0, HALF, lambda c: (w_hi[:, h, which, c, :], w_lo[:, h, which, c, :]),
                               lambda c: (y_hi[:, c, at], y_lo[:, c, at]), CC, begin, end)

            def run(step, psum, begin=0, end=CC):
                kind, h, n = step
                if kind == "q":
                    return project_y(psum, h, Q, n, begin, end)
                if kind == "vt":
                    return project_y(psum, h, V, n)
                if kind == "k":
                    project_y(bank[:, 0, :], h, K, 0)
                    return project_y(bank[:, 1, :], h, K, 1)
                if kind == "turn_v":
                    for i in range(KEYS // 2):
                        c = n * (KEYS // 2) + i
                        done = nc.tensor.transpose(psum[:, i * P:(i + 1) * P], vt[:, c * P:(c + 1) * P], ident[:, :])
                    return done
                if kind == "mean":
                    return nc.tensor.matmul(psum[:, 0:1], average[:, :], part[:, 0:1], start=True, stop=True)
                if kind == "variance":
                    return nc.tensor.matmul(psum[:, 0:1], average[:, :], spread[:, :], start=True, stop=True)
                at = slice(h * HALF, (h + 1) * HALF)
                return product(psum, 0, HALF,
                               lambda c: (wo_hi[:, c, n * P:(n + 1) * P], wo_lo[:, c, n * P:(n + 1) * P]),
                               lambda c: (o_hi[:, c, at], o_lo[:, c, at]), CC, begin, end)

            def score_tile(t):
                s = 2 * (t % 2)
                tile = slice(t * P, (t + 1) * P)
                for half in range(2):
                    at = slice(half * HALF, (half + 1) * HALF)
                    done = product(bank[:, s + half, :], 0, HALF, lambda i: (q_hi[:, tile], q_lo[:, tile]),
                                   lambda i: (k_hi[:, at], k_lo[:, at]), 1)
                return done

            def scores(free_at, unit):
                pe.wait_ge(bank_free, free_at)
                for t in range(TILES):
                    if t >= 2:
                        pe.wait_ge(exp_ready, TILES * unit + t - 1)
                    score_tile(t).then_inc(scores_ready, 1)

            pe.wait_ge(constants_set, 3)
            before = Tally()
            for step in HEAD_START:
                if step[0] == "mean":
                    pe.wait_ge(part_ready, 1)
                elif step[0] == "variance":
                    pe.wait_ge(spread_ready, 1)
                elif step[0] == "vt":
                    pe.wait_ge(weight_split, 1)
                    pe.wait_ge(y_ready, 1)
                elif step[0] == "q":
                    pe.wait_ge(bank_free, 2)
                run(step, psum_of(step, before)).then_inc(ring_ready if in_ring(step) else bank_ready, 1)
                before.add(step)
            scores(START.bank, 0)
            pe.wait_ge(weight_split, HEADS + 1)

            def batch(b, last):
                n = Tally()

                def ring_bank():
                    pe.wait_ge(ring_free, BATCH.ring * b + START.ring + max(n.ring + 1 - RING, 0))
                    return ring[:, (START.ring + n.ring) % RING, :]

                def fill(step, unit, begin=0, end=CC):
                    kind, h, m = step
                    if begin == 0:
                        if in_ring(step):
                            ring_bank()
                        elif min(score_banks(step)) < 2:
                            pe.wait_ge(exp_ready, TILES * unit + TILES - 1)
                        else:
                            pe.wait_ge(exp_ready, TILES * unit + TILES)
                        if kind == "q" and m == 1 and h == 0 or kind == "k" and h == 0:
                            pe.wait_ge(bank_free, START.bank + BATCH.bank * b + n.bank)
                        if kind == "turn_v" and m == 1:
                            pe.wait_ge(ring_free, START.ring + BATCH.ring * b + n.ring - 2)
                        if kind == "vt" and h == 0 and m == 0:
                            pe.wait_ge(y_ready, b + 2)
                        if kind == "mean":
                            pe.wait_ge(part_ready, b + 2)
                        if kind == "variance":
                            pe.wait_ge(spread_ready, b + 2)
                        if kind == "project" and m == 0:
                            pe.wait_ge(attended_free, UNITS * b + (UNITS if h == 0 else UNITS + 1))
                    at_start = Tally()
                    at_start.ring = START.ring + n.ring
                    done = run(step, psum_of(step, at_start), begin, end)
                    if end == CC:
                        done.then_inc(ring_ready if in_ring(step) else bank_ready, 1)
                        n.add(step)

                def turn(c):
                    where = ring_bank()
                    for t in range(TILES):
                        done = nc.tensor.transpose(where[:, t * P:(t + 1) * P], probs[:, t, c * P:(c + 1) * P],
                                                   ident[:, :])
                    done.then_inc(ring_ready, 1)
                    n.add(("turned", 0, c))

                def attend(c, turned_at):
                    pe.wait_ge(ring_free, turned_at)
                    product(attended, 0, HALF, lambda i: (v_hi[:, i, :], v_lo[:, i, :]),
                            lambda i: (turned_hi[:, i % RING, :], turned_lo[:, i % RING, :]), KEYS, c,
                            c + 1).then_inc(attend_done, 1)

                for u in range(UNITS):
                    unit = UNITS * b + u
                    before, slipped, after = fills(u, last)
                    for step in before:
                        fill(step, unit)
                    fill(slipped, unit, 0, CC - 1)
                    pe.wait_ge(probs_ready, TILES * (unit + 1))
                    turned_at = []
                    for c in range(2):
                        turn(c)
                        turned_at.append(START.ring + BATCH.ring * b + n.ring)
                    fill(slipped, unit, CC - 1, CC)
                    for step in after:
                        fill(step, unit)
                    v_at = START.bank + BATCH.bank * b + n.bank - sum(s[0] == "mean" for s in after)
                    pe.wait_ge(attended_free, unit + 1)
                    for c in range(KEYS):
                        if c + 2 < KEYS:
                            turn(c + 2)
                            turned_at.append(START.ring + BATCH.ring * b + n.ring)
                        if c == KEYS // 2 and u % 2 == 0:
                            pe.wait_ge(bank_free, v_at)
                        attend(c, turned_at[c])
                    if u < UNITS - 1 or not last:
                        scores(START.bank + BATCH.bank * b + n.bank, unit + 1)
                for step in TAIL:
                    fill(step, UNITS * b + (UNITS - 1 if last else UNITS))

            with pe.Fori(0, BATCHES - 1) as b:
                batch(b, False)
            batch(BATCHES - 1, True)


def kernel(x, L0_conv_gn_weight, L0_conv_gn_bias, L0_conv_qkv_w, L0_conv_qkv_b, L0_conv_out_w, L0_conv_out_b):
    import numpy as np
    from concourse import bacc
    from concourse.bass_utils import run_bass_kernel_spmd

    def columns(v):
        return np.asarray(v).reshape(-1, P).T

    x = np.asarray(x)
    arrays = {
        "x_dram": np.ascontiguousarray(x.reshape(BATCHES, C, S)),
        "w_qkv_dram": np.ascontiguousarray(
            np.asarray(L0_conv_qkv_w).reshape(3, HEADS, D, CC, P).transpose(4, 1, 0, 3, 2).reshape(P, HEADS, 3 * CC * D)),
        "w_out_dram": np.ascontiguousarray(
            np.asarray(L0_conv_out_w).reshape(C, HEADS, D).transpose(2, 1, 0).reshape(P, HEADS * C)),
        "vectors_dram": np.ascontiguousarray(np.concatenate(
            [columns(L0_conv_gn_weight), columns(L0_conv_gn_bias), columns(L0_conv_qkv_b), columns(L0_conv_out_b)], axis=1)),
    }
    nc = bacc.Bacc("TRN2", target_bir_lowering=False, num_devices=1)
    args = [nc.dram_tensor(name, a.shape, F32, kind="ExternalInput").ap() for name, a in arrays.items()]
    out = nc.dram_tensor("out_dram", (BATCHES, C, S), F32, kind="ExternalOutput").ap()
    attention_program(nc, *args, out)
    r = run_bass_kernel_spmd(nc, [arrays], core_ids=[0])
    return r.results[0]["out_dram"].reshape(x.shape)
```

```python
from contextlib import ExitStack

import concourse.bass as bass
from concourse import mybir

F32 = mybir.dt.float32
F32R = mybir.dt.float32r
ALU = mybir.AluOpType
ACT = mybir.ActivationFunctionType
AX_X = mybir.AxisListType.X

P = 128
BATCHES, C, S = 16, 512, 1024
HEADS = 4
D = C // HEADS
CC = C // P
KEYS = S // P
HALF = 512
TILES = HALF // P
LAST = TILES - 1
FIRST = 2 * P
UNITS = 2 * HEADS
EPS = 1e-5
Q, K, V = 0, 1, 2
RING = 3
HI_SLOTS = 4
BN = 6

GAMMA, BETA, QKV_B, OUT_B = 0, CC, 2 * CC, 2 * CC + 3 * HEADS
VECTORS = OUT_B + CC


def fills(u, last):
    h, half = divmod(u, 2)
    if half == 0:
        after = [("mean", 0, 0)] if u == 4 and not last else []
        return [("vt", h, 1), ("turn_v", h, 0)], ("q", h, 1), [("turn_v", h, 1)], after
    if h < HEADS - 1:
        after = [("variance", 0, 0)] if u == 5 and not last else []
        return [("vt", h + 1, 0), ("q", h + 1, 0)], ("k", h + 1, 0), [], after
    project = [("project", 0, m) for m in range(CC)]
    if last:
        return project[:-1], project[-1], [], []
    return project + [("vt", 0, 0), ("q", 0, 0)], ("k", 0, 0), [], []


def in_ring(step):
    kind, h, n = step
    return kind in ("vt", "turned") or (kind, n) in (("turn_v", 0), ("project", 0)) or (
        kind == "q" and n == 0 and h > 0)


def split_in_two(step):
    return step[0] in ("q", "k", "turn_v", "turned")


def score_banks(step):
    kind, _, n = step
    if kind == "k":
        return 0, 1
    if kind == "q":
        return (0,) if n == 1 else (3,)
    return {"turn_v": (1,), "mean": (2,), "variance": (3,), "project": (n - 1,)}[kind]


class Tally:

    def __init__(self):
        self.ring = self.ring_hi = self.bank = self.bank_hi = 0

    def add(self, step):
        if in_ring(step):
            self.ring += 1
            self.ring_hi += split_in_two(step)
        else:
            self.bank += 1
            self.bank_hi += split_in_two(step)


def results(u, last):
    before, slipped, beside, after = fills(u, last)
    turned = [("turned", 0, c) for c in range(KEYS)]
    early = turned[:RING] + beside + turned[RING:KEYS // 2]
    return before + early + [slipped] + after + turned[KEYS // 2:]


PASSES = 3


def cut(unit):
    return CC * PASSES // 2 + (unit < UNITS - 1)


def slip(step):
    return PASSES if step[0] == "k" else 2 * PASSES


TAIL = [("project", 1, m) for m in range(CC)]
HEAD_START = [("mean", 0, 0), ("variance", 0, 0), ("vt", 0, 0), ("k", 0, 0), ("q", 0, 0)]
START, BATCH = Tally(), Tally()
for _step in HEAD_START:
    START.add(_step)
for _u in range(UNITS):
    for _step in results(_u, False):
        BATCH.add(_step)
for _step in TAIL:
    BATCH.add(_step)
assert BATCH.ring % RING == 0


def attention_program(nc, x, w_qkv, w_out, vectors, out):
    ctx = ExitStack()
    with ctx:
        def sb(name, shape, dt=F32):
            return ctx.enter_context(nc.sbuf_tensor(name, shape, dt))

        def ps(name, shape):
            return ctx.enter_context(nc.psum_tensor(name, shape, F32))

        def sem(name):
            return ctx.enter_context(nc.semaphore(name))

        w_hi = sb("w_hi", [P, HEADS, 3, CC, D], F32R)
        w_lo = sb("w_lo", [P, HEADS, 3, CC, D], F32R)
        wo_hi = sb("wo_hi", [P, HEADS, C], F32R)
        wo_lo = sb("wo_lo", [P, HEADS, C], F32R)
        x_in = sb("x_in", [P, CC, S])
        y_hi = sb("y_hi", [P, CC, S], F32R)
        y_lo = sb("y_lo", [P, CC, S], F32R)
        q_hi = sb("q_hi", [P, HALF], F32R)
        q_lo = sb("q_lo", [P, HALF], F32R)
        k_hi = sb("k_hi", [P, S], F32R)
        k_lo = sb("k_lo", [P, S], F32R)
        vt = sb("vt", [P, S])
        v_hi = sb("v_hi", [P, KEYS, D], F32R)
        v_lo = sb("v_lo", [P, KEYS, D], F32R)
        probs = sb("probs", [P, TILES, S])
        turned_hi = sb("turned_hi", [P, HI_SLOTS, HALF], F32R)
        turned_lo = sb("turned_lo", [P, RING, HALF], F32R)
        o_hi = sb("o_hi", [P, HEADS, S], F32R)
        o_lo = sb("o_lo", [P, HEADS, S], F32R)
        rows = sb("rows", [P, CC, HALF])
        vec = sb("vec", [P, VECTORS])
        ident = sb("ident", [P, P])
        average = sb("average", [P, P])
        minus_half = sb("minus_half", [P, 1])
        bn = sb("bn", [P, 2 * CC, BN])
        part = sb("part", [P, 2])
        neg_mean = sb("neg_mean", [P, 1])
        offset = sb("offset", [P, 1])
        spread = sb("spread", [P, 1])
        variance = sb("variance", [P, 1])
        rstd = sb("rstd", [P, 1])
        gain = sb("gain", [P, CC])
        neg_max = sb("neg_max", [P, TILES])
        row_sum = sb("row_sum", [P, TILES])
        row_scale = sb("row_scale", [P, TILES])

        bank = ps("bank", [P, 4, HALF])
        ring = ps("ring", [P, RING, HALF])
        attended = ps("attended", [P, HALF])

        stage = probs[:, :, :].rearrange("p (s t) n -> p s (t n)", s=2)
        staged = [stage[:, h % 2, 0:3 * CC * D] for h in range(HEADS)]
        staged.append(rows[:, :, :].rearrange("p m n -> p (m n)"))

        vec_loaded = sem("vec_loaded")
        stage_loaded = [sem(f"stage_loaded{i}") for i in range(3)]
        x_loaded = [sem(f"x_loaded{i}") for i in range(CC)]
        rows_loaded = [sem(f"rows_loaded{i}") for i in range(CC)]
        rows_stored = [sem(f"rows_stored{i}") for i in range(CC)]
        constants_set = sem("constants_set")
        ident_cleared = sem("ident_cleared")
        q_bias_scaled = sem("q_bias_scaled")
        weight_hi = sem("weight_hi")
        weight_split = sem("weight_split")
        bn_done = sem("bn_done")
        part_ready = sem("part_ready")
        offset_ready = sem("offset_ready")
        spread_ready = sem("spread_ready")
        rstd_ready = sem("rstd_ready")
        gain_ready = sem("gain_ready")
        normalised = sem("normalised")
        y_hi_ready = sem("y_hi_ready")
        y_ready = sem("y_ready")
        scores_ready = sem("scores_ready")
        max_ready = sem("max_ready")
        exp_ready = sem("exp_ready")
        scale_ready = sem("scale_ready")
        probs_ready = sem("probs_ready")
        last_probs_ready = sem("last_probs_ready")
        ring_ready = sem("ring_ready")
        ring_hi = sem("ring_hi")
        ring_free = sem("ring_free")
        bank_ready = sem("bank_ready")
        bank_hi = sem("bank_hi")
        bank_free = sem("bank_free")
        attend_done = sem("attend_done")
        o_hi_ready = sem("o_hi_ready")
        attended_free = sem("attended_free")
        rows_ready = sem("rows_ready")
        dve_turn = sem("dve_turn")
        pool_turn = sem("pool_turn")

        pieces = [(w_hi[:, h, :, :, :].rearrange("p a c d -> p (a c d)"),
                   w_lo[:, h, :, :, :].rearrange("p a c d -> p (a c d)")) for h in range(HEADS)]
        pieces.append((wo_hi[:, :, :].rearrange("p h n -> p (h n)"),
                       wo_lo[:, :, :].rearrange("p h n -> p (h n)")))
        QUERY = CC * D
        SCALE = float(D) ** -0.5

        def parts(i):
            n = HEADS * C if i == HEADS else 3 * QUERY
            return [(0, n, 1.0)] if i == HEADS else [(0, QUERY, SCALE), (QUERY, n, 1.0)]

        def bias(step):
            kind, h, n = step
            at = {"q": QKV_B + Q * HEADS + h, "k": QKV_B + K * HEADS + h,
                  "vt": QKV_B + V * HEADS + h, "project": OUT_B + n}[kind]
            return vec[:, at:at + 1]

        def psum_of(step, n):
            if in_ring(step):
                return ring[:, n.ring % RING, :]
            banks = score_banks(step)
            if len(banks) == 2:
                return bank[:, 0:2, :].rearrange("p b n -> p (b n)")
            return bank[:, banks[0], :]

        def pair_of(step):
            kind, h, n = step
            if kind == "q":
                return q_hi[:, :], q_lo[:, :]
            if kind == "k":
                return k_hi[:, :], k_lo[:, :]
            if kind == "turn_v":
                a = n * KEYS // 2
                return tuple(v[:, a:a + KEYS // 2, :].rearrange("p c d -> p (c d)") for v in (v_hi, v_lo))
            return turned_hi[:, n % HI_SLOTS, :], turned_lo[:, n % RING, :]

        def x_of(b, m, half):
            return x[b, m * P:(m + 1) * P, half * HALF:(half + 1) * HALF]

        block = ctx.enter_context(nc.Block())

        @block.sync
        def _(sp):
            for c in range(CC):
                sp.dma_start(x_in[:, c, :], x[0, c * P:(c + 1) * P, :]).then_inc(x_loaded[c], 16)
            for i in range(2, HEADS):
                sp.wait_ge(weight_split, i - 1)
                sp.dma_start(staged[i], w_qkv[:, i, :]).then_inc(stage_loaded[i % 2], 16)
            sp.dma_start(staged[HEADS], w_out).then_inc(stage_loaded[2], 16)
            sp.wait_ge(weight_split, HEADS + 1)
            for m in range(CC):
                sp.dma_start(rows[:, m, :], x_of(0, m, 0)).then_inc(rows_loaded[m], 16)

            def batch(b, last):
                if not last:
                    sp.wait_ge(y_ready, b + 1)
                    for c in range(CC):
                        sp.dma_start(x_in[:, c, :], x[b + 1, c * P:(c + 1) * P, :]).then_inc(x_loaded[c], 16)
                for half in range(2):
                    for m in range(CC):
                        sp.wait_ge(rows_ready, 2 * CC * b + CC * half + m + 1)
                        sp.dma_start(out[b, m * P:(m + 1) * P, half * HALF:(half + 1) * HALF],
                                     rows[:, m, :]).then_inc(rows_stored[m], 16)
                    if half == 1 and last:
                        continue
                    for m in range(CC):
                        sp.wait_ge(rows_stored[m], 32 * b + 16 * half + 16)
                        sp.dma_start(rows[:, m, :], x_of(b + half, m, 1 - half)).then_inc(rows_loaded[m], 16)

            with sp.Fori(0, BATCHES - 1) as b:
                batch(b, False)
            batch(BATCHES - 1, True)
            for m in range(CC):
                sp.wait_ge(rows_stored[m], 32 * BATCHES)

        @block.gpsimd
        def _(pool):
            pool.memset(ident[:, :], 0.0).then_inc(ident_cleared, 1)
            pool.memset(average[:, :], 1.0 / P).then_inc(constants_set, 1)
            pool.memset(minus_half[:, :], -0.5).then_inc(constants_set, 1)
            pool.wait_ge(ident_cleared, 1)
            pool.affine_select(out=ident[:, :], in_=ident[:, :], compare_op=ALU.not_equal, fill=1.0, base=0,
                               pattern=[[-1, P]], channel_multiplier=1).then_inc(constants_set, 1)

            def hold(semaphore, value):
                pool.wait_ge(semaphore, value)
                pool.sem_inc(pool_turn, 1)

            def normalise(b, variance_at):
                pool.wait_ge(bank_free, variance_at)
                pool.tensor_tensor(rstd[:, :], variance[:, :], minus_half[:, :], ALU.pow).then_inc(rstd_ready, 1)
                pool.wait_ge(rstd_ready, b + 1)
                pool.tensor_tensor(gain[:, :], vec[:, GAMMA:GAMMA + CC], rstd[:, 0:1].broadcast_to([P, CC]),
                                   ALU.mult).then_inc(gain_ready, 1)
                hold(gain_ready, b + 1)
                for c in range(CC):
                    pool.tensor_scalar(x_in[:, c, :], x_in[:, c, :], neg_mean[:, 0:1], gain[:, c:c + 1],
                                       ALU.add, ALU.mult).then_inc(normalised, 1)

            def scale_rows(unit):
                for t in range(LAST):
                    hold(scale_ready, TILES * unit + t + 1)
                    pool.tensor_scalar(probs[:, t, :], probs[:, t, :], row_scale[:, t:t + 1], 1.0,
                                       ALU.mult, ALU.mult).then_inc(probs_ready, 1)

            pool.wait_ge(constants_set, 3)
            pool.wait_ge(vec_loaded, 16)
            normalise(0, 2)
            scale_rows(0)

            def batch(b, last):
                n = Tally()
                for u in range(UNITS):
                    for step in results(u, last):
                        n.add(step)
                        if step[0] == "variance":
                            variance_at = START.bank + BATCH.bank * b + n.bank
                    if u == 5 and not last:
                        normalise(b + 1, variance_at)
                    if u < UNITS - 1 or not last:
                        scale_rows(UNITS * b + u + 1)

            with pool.Fori(0, BATCHES - 1) as b:
                batch(b, False)
            batch(BATCHES - 1, True)

        @block.scalar
        def _(act):
            act.dma_start(vec[:, :], vectors).then_inc(vec_loaded, 16)
            for i in range(2):
                act.dma_start(staged[i], w_qkv[:, i, :]).then_inc(stage_loaded[i], 16)

            def weights(i):
                if i < HEADS:
                    act.wait_ge(stage_loaded[i % 2], 16 * (i // 2 + 1))
                else:
                    act.wait_ge(stage_loaded[2], 16)
                for a, z, factor in parts(i):
                    act.activation(pieces[i][0][:, a:z], staged[i][:, a:z], ACT.Copy,
                                   scale=factor).then_inc(weight_hi, 1)

            def y_parts(b):
                for c in range(CC):
                    act.wait_ge(normalised, CC * b + c + 1)
                    act.activation(y_hi[:, c, :], x_in[:, c, :], ACT.Identity,
                                   bias=vec[:, BETA + c:BETA + c + 1]).then_inc(y_hi_ready, 1)

            def hi_part(step, b, n):
                if in_ring(step):
                    act.wait_ge(ring_ready, START.ring + BATCH.ring * b + n.ring + 1)
                    done = ring_hi
                else:
                    act.wait_ge(bank_ready, START.bank + BATCH.bank * b + n.bank + 1)
                    done = bank_hi
                if step[0] in ("q", "k"):
                    act.activation(pair_of(step)[0], psum(step, n), ACT.Identity, bias=bias(step)).then_inc(done, 1)
                else:
                    act.activation(pair_of(step)[0], psum(step, n), ACT.Copy).then_inc(done, 1)

            def psum(step, n):
                n.ring += START.ring
                where = psum_of(step, n)
                n.ring -= START.ring
                return where

            def exponentials(unit, turned=None):
                for t in range(TILES):
                    if turned is not None and t == 0:
                        act.wait_ge(ring_ready, turned)
                    act.wait_ge(max_ready, TILES * unit + t + 1)
                    s = 2 * (t % 2)
                    act.activation(probs[:, t, :], bank[:, s:s + 2, :].rearrange("p b n -> p (b n)"), ACT.Exp,
                                   bias=neg_max[:, t:t + 1], accum_out=row_sum[:, t:t + 1]).then_inc(exp_ready, 1)

            weights(0)
            weights(1)
            y_parts(0)
            weights(2)
            weights(3)
            act.wait_ge(q_bias_scaled, 1)
            before = Tally()
            for step in HEAD_START:
                if split_in_two(step):
                    act.wait_ge(bank_ready, before.bank + 1)
                    act.activation(pair_of(step)[0], psum_of(step, before), ACT.Identity,
                                   bias=bias(step)).then_inc(bank_hi, 1)
                before.add(step)
            act.wait_ge(weight_split, HEADS)
            exponentials(0)
            weights(HEADS)

            def batch(b, last):
                n = Tally()
                for u in range(UNITS):
                    h, half = divmod(u, 2)
                    if u == UNITS - 1 and not last:
                        y_parts(b + 1)
                    for step in results(u, last):
                        if step[0] == "turned" and step[2] >= HI_SLOTS:
                            act.wait_ge(attend_done, KEYS * (UNITS * b + u) + step[2] - HI_SLOTS + 1)
                        if split_in_two(step):
                            hi_part(step, b, n)
                        n.add(step)
                    act.wait_ge(attend_done, KEYS * (UNITS * b + u + 1))
                    act.activation(o_hi[:, h, half * HALF:(half + 1) * HALF], attended[:, :],
                                   ACT.Copy).then_inc(o_hi_ready, 1)
                    if u < UNITS - 1 or not last:
                        exponentials(UNITS * b + u + 1, START.ring + BATCH.ring * b + n.ring)

            with act.Fori(0, BATCHES - 1) as b:
                batch(b, False)
            batch(BATCHES - 1, True)

        @block.vector
        def _(dve):
            def weights(i):
                for n, (a, z, factor) in enumerate(parts(i)):
                    dve.wait_ge(weight_hi, 2 * i + n + 1)
                    lo = dve.scalar_tensor_tensor(pieces[i][1][:, a:z], staged[i][:, a:z], factor,
                                                  pieces[i][0][:, a:z].bitcast(F32), ALU.mult, ALU.subtract)
                lo.then_inc(weight_split, 1)

            def partition_statistics(b, before_last=lambda: None):
                for c in range(CC):
                    if c == CC - 1:
                        before_last()
                    dve.wait_ge(x_loaded[c], 16 * b + 16)
                    for half in range(2):
                        dve.bn_stats(bn[:, 2 * c + half, :],
                                     x_in[:, c, half * HALF:(half + 1) * HALF]).then_inc(bn_done, 1)
                dve.wait_ge(bn_done, 2 * CC * (b + 1))
                dve.sem_inc(dve_turn, 1)
                dve.bn_aggr(part[:, :], bn[:, :, :].rearrange("p a s -> p (a s)")).then_inc(part_ready, 1)

            def whole_mean(b, psum, ready_at):
                dve.wait_ge(bank_ready, ready_at)
                dve.tensor_scalar(neg_mean[:, :], psum[:, 0:1], -1.0, None, ALU.mult).then_inc(bank_free, 1)
                dve.wait_ge(bank_free, ready_at)
                dve.tensor_tensor(offset[:, :], part[:, 0:1], neg_mean[:, :], ALU.add).then_inc(offset_ready, 1)
                dve.wait_ge(offset_ready, b + 1)
                dve.scalar_tensor_tensor(spread[:, :], offset[:, :], offset[:, 0:1], part[:, 1:2], ALU.mult,
                                         ALU.add).then_inc(spread_ready, 1)

            def whole_variance(psum, ready_at):
                dve.wait_ge(bank_ready, ready_at)
                dve.tensor_scalar(variance[:, :], psum[:, 0:1], EPS, None, ALU.add).then_inc(bank_free, 1)

            def y_parts(b):
                for c in range(CC):
                    dve.wait_ge(y_hi_ready, CC * b + c + 1)
                    lo = dve.scalar_tensor_tensor(y_lo[:, c, :], x_in[:, c, :], vec[:, BETA + c:BETA + c + 1],
                                                  y_hi[:, c, :].bitcast(F32), ALU.add, ALU.subtract)
                lo.then_inc(y_ready, 1)

            def softmax(unit, first_result=lambda: None):
                def maximum(t):
                    dve.wait_ge(scores_ready, TILES * unit + t + 1)
                    s = 2 * (t % 2)
                    dve.tensor_reduce(neg_max[:, t:t + 1], bank[:, s:s + 2, :].rearrange("p b n -> p (b n)"),
                                      AX_X, ALU.max, negate=True).then_inc(max_ready, 1)

                def inverse(t):
                    dve.wait_ge(exp_ready, TILES * unit + t + 1)
                    dve.reciprocal(row_scale[:, t:t + 1], row_sum[:, t:t + 1]).then_inc(scale_ready, 1)

                for t in range(TILES):
                    maximum(t)
                    if t == 1:
                        inverse(0)
                        inverse(1)
                inverse(2)
                first_result()
                inverse(LAST)
                dve.wait_ge(scale_ready, TILES * (unit + 1))
                for a, z in ((0, FIRST), (FIRST, S)):
                    dve.tensor_scalar(probs[:, LAST, a:z], probs[:, LAST, a:z], row_scale[:, LAST:TILES], None,
                                      ALU.mult).then_inc(last_probs_ready, 1)

            def finish(step, b, n, start=START):
                kind, h, m = step
                ring_at = start.ring + BATCH.ring * b + n.ring + 1
                bank_at = start.bank + BATCH.bank * b + n.bank + 1
                at_start = Tally()
                at_start.ring = start.ring + n.ring
                psum = psum_of(step, at_start)
                free = ring_free if in_ring(step) else bank_free
                if kind == "mean":
                    whole_mean(b + (start is START), psum, bank_at)
                elif kind == "variance":
                    whole_variance(psum, bank_at)
                elif split_in_two(step):
                    hi, lo = pair_of(step)
                    if in_ring(step):
                        dve.wait_ge(ring_hi, BATCH.ring_hi * b + n.ring_hi + 1)
                    else:
                        dve.wait_ge(bank_hi, start.bank_hi + BATCH.bank_hi * b + n.bank_hi + 1)
                    if kind in ("q", "k"):
                        dve.scalar_tensor_tensor(lo, psum, bias(step), hi.bitcast(F32), ALU.add,
                                                 ALU.subtract).then_inc(free, 1)
                    else:
                        dve.tensor_tensor(lo, psum, hi.bitcast(F32), ALU.subtract).then_inc(free, 1)
                elif kind == "vt":
                    dve.wait_ge(ring_ready, ring_at)
                    dve.tensor_scalar(vt[:, m * HALF:(m + 1) * HALF], psum, bias(step), None,
                                      ALU.add).then_inc(free, 1)
                else:
                    if in_ring(step):
                        dve.wait_ge(ring_ready, ring_at)
                    else:
                        dve.wait_ge(bank_ready, bank_at)
                    dve.wait_ge(rows_loaded[m], 32 * b + 16 * h + 16)
                    dve.scalar_tensor_tensor(rows[:, m, :], psum, bias(step), rows[:, m, :], ALU.add,
                                             ALU.add).then_inc(rows_ready, 1)
                    dve.wait_ge(rows_ready, 2 * CC * b + CC * h + m + 1)
                    dve.sem_inc(free, 1)

            dve.wait_ge(vec_loaded, 16)
            dve.tensor_scalar(vec[:, QKV_B:QKV_B + HEADS], vec[:, QKV_B:QKV_B + HEADS], SCALE, None,
                              ALU.mult).then_inc(q_bias_scaled, 1)
            dve.memset(offset[:, :], 0.0).then_inc(attended_free, 1)
            partition_statistics(0, lambda: weights(0))
            before = Tally()
            for step in HEAD_START[:2]:
                finish(step, 0, before, Tally())
                before.add(step)
            weights(1)
            y_parts(0)
            weights(2)
            weights(3)
            for step in HEAD_START[2:]:
                finish(step, 0, before, Tally())
                before.add(step)
            softmax(0)
            weights(HEADS)

            def batch(b, last):
                n = Tally()

                def take(step):
                    finish(step, b, n)
                    n.add(step)

                for u in range(UNITS):
                    h, half = divmod(u, 2)
                    if u == 3 and not last:
                        partition_statistics(b + 1)
                    if u == UNITS - 1 and not last:
                        y_parts(b + 1)
                    for step in results(u, last)[1 if u > 0 else 0:]:
                        if step[0] == "turned" and step[2] >= RING:
                            dve.wait_ge(attend_done, KEYS * (UNITS * b + u) + step[2] - RING + 1)
                        take(step)
                    dve.wait_ge(o_hi_ready, UNITS * b + u + 1)
                    at = slice(half * HALF, (half + 1) * HALF)
                    dve.tensor_tensor(o_lo[:, h, at], attended[:, :], o_hi[:, h, at].bitcast(F32),
                                      ALU.subtract).then_inc(attended_free, 1)
                    first = results(u + 1, last)[0] if u < UNITS - 1 else TAIL[0]
                    if u < UNITS - 1 or not last:
                        softmax(UNITS * b + u + 1, lambda: take(first))
                for step in TAIL[0 if last else 1:]:
                    take(step)

            with dve.Fori(0, BATCHES - 1) as b:
                batch(b, False)
            batch(BATCHES - 1, True)

        @block.tensor
        def _(pe):
            def product(psum, a, z, stationary, moving, contractions, begin=0, end=None):
                last = PASSES * contractions - 1
                for m in range(begin, last + 1 if end is None else end):
                    i, which = divmod(m, PASSES)
                    s_hi, s_lo = stationary(i)
                    m_hi, m_lo = moving(i)
                    left, right = ((s_hi, m_hi), (s_hi, m_lo), (s_lo, m_hi))[which]
                    done = nc.tensor.matmul(psum[:, a:z], left, right, start=(m == 0), stop=(m == last))
                return done

            def project_y(psum, h, which, half, begin=0, end=None):
                at = slice(half * HALF, (half + 1) * HALF)
                return product(psum, 0, HALF, lambda c: (w_hi[:, h, which, c, :], w_lo[:, h, which, c, :]),
                               lambda c: (y_hi[:, c, at], y_lo[:, c, at]), CC, begin, end)

            def run(step, psum, begin=0, end=CC * PASSES):
                kind, h, n = step
                if kind == "q":
                    return project_y(psum, h, Q, n, begin, end)
                if kind == "vt":
                    return project_y(psum, h, V, n, begin, end)
                if kind == "k":
                    project_y(bank[:, 0, :], h, K, 0, begin, end)
                    return project_y(bank[:, 1, :], h, K, 1, begin, end)
                if kind == "turn_v":
                    for i in range(KEYS // 2):
                        c = n * (KEYS // 2) + i
                        done = nc.tensor.transpose(psum[:, i * P:(i + 1) * P], vt[:, c * P:(c + 1) * P], ident[:, :])
                    return done
                if kind == "mean":
                    return nc.tensor.matmul(psum[:, 0:1], average[:, :], part[:, 0:1], start=True, stop=True)
                if kind == "variance":
                    return nc.tensor.matmul(psum[:, 0:1], average[:, :], spread[:, :], start=True, stop=True)
                at = slice(h * HALF, (h + 1) * HALF)
                return product(psum, 0, HALF,
                               lambda c: (wo_hi[:, c, n * P:(n + 1) * P], wo_lo[:, c, n * P:(n + 1) * P]),
                               lambda c: (o_hi[:, c, at], o_lo[:, c, at]), CC, begin, end)

            def score_tile(t):
                s = 2 * (t % 2)
                tile = slice(t * P, (t + 1) * P)
                for half in range(2):
                    at = slice(half * HALF, (half + 1) * HALF)
                    done = product(bank[:, s + half, :], 0, HALF, lambda i: (q_hi[:, tile], q_lo[:, tile]),
                                   lambda i: (k_hi[:, at], k_lo[:, at]), 1)
                return done

            def scores(free_at, unit, begin_fill=lambda: None):
                pe.wait_ge(bank_free, free_at)
                for t in range(TILES):
                    if t == 2:
                        begin_fill()
                    if t >= 2:
                        pe.wait_ge(exp_ready, TILES * unit + t - 1)
                    score_tile(t).then_inc(scores_ready, 1)

            pe.wait_ge(constants_set, 3)
            before = Tally()
            for step in HEAD_START:
                if step[0] == "mean":
                    pe.wait_ge(part_ready, 1)
                elif step[0] == "variance":
                    pe.wait_ge(spread_ready, 1)
                elif step[0] == "vt":
                    pe.wait_ge(weight_split, 1)
                    pe.wait_ge(y_ready, 1)
                elif step[0] == "q":
                    pe.wait_ge(bank_free, 2)
                run(step, psum_of(step, before)).then_inc(ring_ready if in_ring(step) else bank_ready, 1)
                before.add(step)
            scores(START.bank, 0)
            pe.wait_ge(weight_split, HEADS)

            def batch(b, last):
                n = Tally()

                def ring_bank():
                    pe.wait_ge(ring_free, BATCH.ring * b + START.ring + max(n.ring + 1 - RING, 0))
                    return ring[:, (START.ring + n.ring) % RING, :]

                def fill(step, unit, begin=0, end=CC * PASSES):
                    kind, h, m = step
                    if begin == 0:
                        if in_ring(step):
                            ring_bank()
                        elif min(score_banks(step)) < 2:
                            pe.wait_ge(exp_ready, TILES * unit + TILES - 1)
                        else:
                            pe.wait_ge(exp_ready, TILES * unit + TILES)
                        if kind == "q" and m == 1 and h == 0:
                            pe.wait_ge(bank_free, START.bank + BATCH.bank * b + n.bank)
                        if kind == "k" and h == 0:
                            pe.wait_ge(bank_free, START.bank + BATCH.bank * b + n.bank - 1)
                        if kind == "turn_v" and m == 1:
                            pe.wait_ge(ring_free, START.ring + BATCH.ring * b + n.ring - 1)
                        if kind == "vt" and h == 0 and m == 0:
                            pe.wait_ge(y_ready, b + 2)
                        if kind == "mean":
                            pe.wait_ge(part_ready, b + 2)
                        if kind == "variance":
                            pe.wait_ge(spread_ready, b + 2)
                        if kind == "project" and m == 0 and not isinstance(b, int):
                            pe.wait_ge(weight_split, HEADS + 1)
                        if kind == "project" and m == 0:
                            pe.wait_ge(attended_free, UNITS * b + (UNITS if h == 0 else UNITS + 1))
                    at_start = Tally()
                    at_start.ring = START.ring + n.ring
                    done = run(step, psum_of(step, at_start), begin, end)
                    if end == CC * PASSES:
                        done.then_inc(ring_ready if in_ring(step) else bank_ready, 1)
                        n.add(step)

                def turn(c):
                    where = ring_bank()
                    if c == FIRST // P:
                        pe.wait_ge(last_probs_ready, 2 * unit + 2)
                    for t in range(TILES):
                        done = nc.tensor.transpose(where[:, t * P:(t + 1) * P], probs[:, t, c * P:(c + 1) * P],
                                                   ident[:, :])
                    done.then_inc(ring_ready, 1)
                    n.add(("turned", 0, c))

                def turn_first(unit):
                    wheres, counts = [], []
                    for c in range(2):
                        wheres.append(ring_bank())
                        n.add(("turned", 0, c))
                        counts.append(START.ring + BATCH.ring * b + n.ring)
                    pe.wait_ge(probs_ready, LAST * (unit + 1))
                    for t in range(TILES):
                        if t == LAST:
                            pe.wait_ge(last_probs_ready, 2 * unit + 1)
                        for c in range(2):
                            done = nc.tensor.transpose(wheres[c][:, t * P:(t + 1) * P],
                                                       probs[:, t, c * P:(c + 1) * P], ident[:, :])
                            if t == LAST:
                                done.then_inc(ring_ready, 1)
                    return counts

                def attend(c, turned_at):
                    pe.wait_ge(ring_free, turned_at)
                    product(attended, 0, HALF, lambda i: (v_hi[:, i, :], v_lo[:, i, :]),
                            lambda i: (turned_hi[:, i % HI_SLOTS, :], turned_lo[:, i % RING, :]), KEYS, PASSES * c,
                            PASSES * (c + 1)).then_inc(attend_done, 1)

                for u in range(UNITS):
                    unit = UNITS * b + u
                    before, slipped, beside, after = fills(u, last)
                    for i, step in enumerate(before):
                        fill(step, unit, cut(u) if i == 0 and u > 0 else 0)
                    fill(slipped, unit, 0, CC * PASSES - slip(slipped))
                    for step in beside:
                        fill(step, unit)
                        v_at = START.bank + BATCH.bank * b + n.bank
                    turned_at = turn_first(unit)

                    def turn_next():
                        turn(len(turned_at))
                        turned_at.append(START.ring + BATCH.ring * b + n.ring)

                    fill(slipped, unit, CC * PASSES - slip(slipped))
                    for step in after:
                        fill(step, unit)
                    turn_next()
                    pe.wait_ge(attended_free, unit + 1)
                    for c in range(KEYS):
                        if len(turned_at) < KEYS:
                            turn_next()
                        if c == KEYS // 2 and u % 2 == 0:
                            pe.wait_ge(bank_free, v_at)
                        attend(c, turned_at[c])
                    if u < UNITS - 1:
                        first = fills(u + 1, last)[0][0]
                    else:
                        first = TAIL[0]
                    if u < UNITS - 1 or not last:
                        scores(START.bank + BATCH.bank * b + n.bank, unit + 1,
                               lambda: fill(first, unit + 1, 0, cut(u + 1)))
                for i, step in enumerate(TAIL):
                    fill(step, UNITS * b + (UNITS - 1 if last else UNITS), cut(UNITS) if i == 0 and not last else 0)

            with pe.Fori(0, BATCHES - 1) as b:
                batch(b, False)
            batch(BATCHES - 1, True)


def kernel(x, L0_conv_gn_weight, L0_conv_gn_bias, L0_conv_qkv_w, L0_conv_qkv_b, L0_conv_out_w, L0_conv_out_b):
    import numpy as np
    from concourse import bacc
    from concourse.bass_utils import run_bass_kernel_spmd

    def columns(v):
        return np.asarray(v).reshape(-1, P).T

    x = np.asarray(x)
    arrays = {
        "x_dram": np.ascontiguousarray(x.reshape(BATCHES, C, S)),
        "w_qkv_dram": np.ascontiguousarray(
            np.asarray(L0_conv_qkv_w).reshape(3, HEADS, D, CC, P).transpose(4, 1, 0, 3, 2).reshape(P, HEADS, 3 * CC * D)),
        "w_out_dram": np.ascontiguousarray(
            np.asarray(L0_conv_out_w).reshape(C, HEADS, D).transpose(2, 1, 0).reshape(P, HEADS * C)),
        "vectors_dram": np.ascontiguousarray(np.concatenate(
            [columns(L0_conv_gn_weight), columns(L0_conv_gn_bias), columns(L0_conv_qkv_b), columns(L0_conv_out_b)], axis=1)),
    }
    nc = bacc.Bacc("TRN2", target_bir_lowering=False, num_devices=1)
    args = [nc.dram_tensor(name, a.shape, F32, kind="ExternalInput").ap() for name, a in arrays.items()]
    out = nc.dram_tensor("out_dram", (BATCHES, C, S), F32, kind="ExternalOutput").ap()
    attention_program(nc, *args, out)
    r = run_bass_kernel_spmd(nc, [arrays], core_ids=[0])
    return r.results[0]["out_dram"].reshape(x.shape)
```

```python
from contextlib import ExitStack

import concourse.bass as bass
from concourse import mybir

F32 = mybir.dt.float32
F32R = mybir.dt.float32r
ALU = mybir.AluOpType
ACT = mybir.ActivationFunctionType
AX_X = mybir.AxisListType.X

P = 128
BATCHES, C, S = 16, 512, 1024
HEADS = 4
D = C // HEADS
CC = C // P
KEYS = S // P
HALF = 512
TILES = HALF // P
LAST = TILES - 1
FIRST = 2 * P
UNITS = 2 * HEADS
EPS = 1e-5
Q, K, V = 0, 1, 2
RING = 3
HI_SLOTS = 4
BN = 6

GAMMA, BETA, QKV_B, OUT_B = 0, CC, 2 * CC, 2 * CC + 3 * HEADS
VECTORS = OUT_B + CC


def fills(u, last):
    h, half = divmod(u, 2)
    if half == 0:
        after = [("mean", 0, 0)] if u == 4 and not last else []
        return [("vt", h, 1), ("turn_v", h, 0)], ("q", h, 1), [("turn_v", h, 1)], after
    if h < HEADS - 1:
        after = [("variance", 0, 0)] if u == 5 and not last else []
        return [("vt", h + 1, 0), ("q", h + 1, 0)], ("k", h + 1, 0), [], after
    project = [("project", 0, m) for m in range(CC)]
    if last:
        return project[:-1], project[-1], [], []
    return project + [("vt", 0, 0), ("q", 0, 0)], ("k", 0, 0), [], []


def in_ring(step):
    kind, h, n = step
    return kind in ("vt", "turned") or (kind, n) in (("turn_v", 0), ("q", 0), ("project", 0), ("project", 1))


def split_in_two(step):
    return step[0] in ("q", "k", "turn_v", "turned")


def score_banks(step):
    kind, _, n = step
    if kind == "k":
        return 0, 1
    return {"q": (0,), "turn_v": (1,), "mean": (2,), "variance": (3,), "project": (n - 2,)}[kind]


class Tally:

    def __init__(self):
        self.ring = self.ring_hi = self.bank = self.bank_hi = 0

    def add(self, step):
        if in_ring(step):
            self.ring += 1
            self.ring_hi += split_in_two(step)
        else:
            self.bank += 1
            self.bank_hi += split_in_two(step)


def results(u, last):
    before, slipped, beside, after = fills(u, last)
    turned = [("turned", 0, c) for c in range(KEYS)]
    early = turned[:RING] + beside + turned[RING:KEYS // 2]
    return before + early + [slipped] + turned[KEYS // 2:-2] + after + turned[-2:]


PASSES = 3

CUT = CC * PASSES // 2 + 1

NO_LAST_HEAD = (HEADS - 1) * PASSES


def slip(step):
    return PASSES if step[0] == "k" else 2 * PASSES


TAIL = [("project", 1, m) for m in range(CC)]
HEAD_START = [("mean", 0, 0), ("variance", 0, 0), ("k", 0, 0), ("q", 0, 0), ("vt", 0, 0)]
START, BATCH = Tally(), Tally()
for _step in HEAD_START:
    START.add(_step)
for _u in range(UNITS):
    for _step in results(_u, False):
        BATCH.add(_step)
for _step in TAIL:
    BATCH.add(_step)
assert BATCH.ring % RING == 0


def attention_program(nc, x, w_qkv, w_out, vectors, out):
    ctx = ExitStack()
    with ctx:
        def sb(name, shape, dt=F32):
            return ctx.enter_context(nc.sbuf_tensor(name, shape, dt))

        def ps(name, shape):
            return ctx.enter_context(nc.psum_tensor(name, shape, F32))

        def sem(name):
            return ctx.enter_context(nc.semaphore(name))

        w_hi = sb("w_hi", [P, HEADS, 3, CC, D], F32R)
        w_lo = sb("w_lo", [P, HEADS, 3, CC, D], F32R)
        wo_hi = sb("wo_hi", [P, HEADS, C], F32R)
        wo_lo = sb("wo_lo", [P, HEADS, C], F32R)
        x_in = sb("x_in", [P, CC, S])
        y_hi = sb("y_hi", [P, CC, S], F32R)
        y_lo = sb("y_lo", [P, CC, S], F32R)
        q_hi = sb("q_hi", [P, HALF], F32R)
        q_lo = sb("q_lo", [P, HALF], F32R)
        k_hi = sb("k_hi", [P, S], F32R)
        k_lo = sb("k_lo", [P, S], F32R)
        vt = sb("vt", [P, S])
        v_hi = sb("v_hi", [P, KEYS, D], F32R)
        v_lo = sb("v_lo", [P, KEYS, D], F32R)
        probs = sb("probs", [P, TILES, S])
        turned_hi = sb("turned_hi", [P, HI_SLOTS, HALF], F32R)
        turned_lo = sb("turned_lo", [P, RING, HALF], F32R)
        o_hi = sb("o_hi", [P, HEADS, S], F32R)
        o_lo = sb("o_lo", [P, HEADS, S], F32R)
        rows = sb("rows", [P, CC, HALF])
        vec = sb("vec", [P, VECTORS])
        ident = sb("ident", [P, P])
        average = sb("average", [P, P])
        minus_half = sb("minus_half", [P, 1])
        bn = sb("bn", [P, 2 * CC, BN])
        part = sb("part", [P, 2])
        neg_mean = sb("neg_mean", [P, 1])
        offset = sb("offset", [P, 1])
        spread = sb("spread", [P, 1])
        variance = sb("variance", [P, 1])
        rstd = sb("rstd", [P, 1])
        gain = sb("gain", [P, CC])
        neg_max = sb("neg_max", [P, TILES])
        row_sum = sb("row_sum", [P, TILES])
        row_scale = sb("row_scale", [P, TILES])

        bank = ps("bank", [P, 4, HALF])
        ring = ps("ring", [P, RING, HALF])
        attended = ps("attended", [P, HALF])

        stage = probs[:, :, :].rearrange("p (s t) n -> p s (t n)", s=2)
        PIECE = 3 * CC * D
        staged = [stage[:, h % 2, 0:PIECE] for h in range(HEADS)]
        staged.append(rows[:, :, :].rearrange("p m n -> p (m n)"))

        vec_loaded = sem("vec_loaded")
        stage_loaded = [sem(f"stage_loaded{i}") for i in range(HEADS + 1)]
        x_loaded = [sem(f"x_loaded{i}") for i in range(CC)]
        rows_loaded = [sem(f"rows_loaded{i}") for i in range(CC)]
        rows_stored = [sem(f"rows_stored{i}") for i in range(CC)]
        constants_set = sem("constants_set")
        ident_cleared = sem("ident_cleared")
        q_bias_scaled = sem("q_bias_scaled")
        weight_scaled = sem("weight_scaled")
        weight_hi = sem("weight_hi")
        weight_split_dve = sem("weight_split_dve")
        weight_split_pool = sem("weight_split_pool")
        bn_done = sem("bn_done")
        part_ready = sem("part_ready")
        offset_ready = sem("offset_ready")
        spread_ready = sem("spread_ready")
        rstd_ready = sem("rstd_ready")
        gain_ready = sem("gain_ready")
        normalised = sem("normalised")
        y_hi_ready = sem("y_hi_ready")
        y_ready = sem("y_ready")
        scores_ready = sem("scores_ready")
        max_ready = sem("max_ready")
        exp_ready = sem("exp_ready")
        scale_ready = sem("scale_ready")
        probs_ready = sem("probs_ready")
        last_probs_ready = sem("last_probs_ready")
        ring_ready = sem("ring_ready")
        ring_hi = sem("ring_hi")
        ring_free = sem("ring_free")
        bank_ready = sem("bank_ready")
        bank_hi = sem("bank_hi")
        bank_free = sem("bank_free")
        attend_done = sem("attend_done")
        o_hi_ready = sem("o_hi_ready")
        attended_free = sem("attended_free")
        rows_ready = sem("rows_ready")
        dve_turn = sem("dve_turn")
        pool_turn = sem("pool_turn")

        pieces = [(w_hi[:, h, :, :, :].rearrange("p a c d -> p (a c d)"),
                   w_lo[:, h, :, :, :].rearrange("p a c d -> p (a c d)")) for h in range(HEADS)]
        pieces.append((wo_hi[:, :, :].rearrange("p h n -> p (h n)"),
                       wo_lo[:, :, :].rearrange("p h n -> p (h n)")))
        QUERY = CC * D
        SCALE = float(D) ** -0.5

        DVE_PIECES, POOL_PIECES = (0, 1, 2), (3, HEADS)

        def hi_written(i):
            return 2 * HEADS + 1 if i == HEADS else 2 * (i + 1)

        def bias(step):
            kind, h, n = step
            at = {"q": QKV_B + Q * HEADS + h, "k": QKV_B + K * HEADS + h,
                  "vt": QKV_B + V * HEADS + h, "project": OUT_B + n}[kind]
            return vec[:, at:at + 1]

        def psum_of(step, n):
            if in_ring(step):
                return ring[:, n.ring % RING, :]
            banks = score_banks(step)
            if len(banks) == 2:
                return bank[:, 0:2, :].rearrange("p b n -> p (b n)")
            return bank[:, banks[0], :]

        def pair_of(step):
            kind, h, n = step
            if kind == "q":
                return q_hi[:, :], q_lo[:, :]
            if kind == "k":
                return k_hi[:, :], k_lo[:, :]
            if kind == "turn_v":
                a = n * KEYS // 2
                return tuple(v[:, a:a + KEYS // 2, :].rearrange("p c d -> p (c d)") for v in (v_hi, v_lo))
            return turned_hi[:, n % HI_SLOTS, :], turned_lo[:, n % RING, :]

        def x_of(b, m, half):
            return x[b, m * P:(m + 1) * P, half * HALF:(half + 1) * HALF]

        block = ctx.enter_context(nc.Block())

        @block.sync
        def _(sp):
            for c in range(CC):
                sp.dma_start(x_in[:, c, :], x[0, c * P:(c + 1) * P, :]).then_inc(x_loaded[c], 16)
            for i in range(HEADS):
                if i >= 2:
                    sp.wait_ge(weight_split_dve, i - 1)
                sp.dma_start(staged[i], w_qkv[:, i, :]).then_inc(stage_loaded[i], 16)
            sp.dma_start(staged[HEADS], w_out).then_inc(stage_loaded[HEADS], 16)
            sp.wait_ge(weight_split_pool, len(POOL_PIECES))
            for m in range(CC):
                sp.dma_start(rows[:, m, :], x_of(0, m, 0)).then_inc(rows_loaded[m], 16)

            def batch(b, last):
                if not last:
                    sp.wait_ge(y_ready, CC * (b + 1))
                    for c in range(CC):
                        sp.dma_start(x_in[:, c, :], x[b + 1, c * P:(c + 1) * P, :]).then_inc(x_loaded[c], 16)
                for half in range(2):
                    for m in range(CC):
                        sp.wait_ge(rows_ready, 2 * CC * b + CC * half + m + 1)
                        sp.dma_start(out[b, m * P:(m + 1) * P, half * HALF:(half + 1) * HALF],
                                     rows[:, m, :]).then_inc(rows_stored[m], 16)
                    if half == 1 and last:
                        continue
                    for m in range(CC):
                        sp.wait_ge(rows_stored[m], 32 * b + 16 * half + 16)
                        sp.dma_start(rows[:, m, :], x_of(b + half, m, 1 - half)).then_inc(rows_loaded[m], 16)

            with sp.Fori(0, BATCHES - 1) as b:
                batch(b, False)
            batch(BATCHES - 1, True)
            for m in range(CC):
                sp.wait_ge(rows_stored[m], 32 * BATCHES)

        @block.gpsimd
        def _(pool):
            pool.memset(ident[:, :], 0.0).then_inc(ident_cleared, 1)
            pool.memset(average[:, :], 1.0 / P).then_inc(constants_set, 1)
            pool.memset(minus_half[:, :], -0.5).then_inc(constants_set, 1)
            pool.wait_ge(ident_cleared, 1)
            pool.affine_select(out=ident[:, :], in_=ident[:, :], compare_op=ALU.not_equal, fill=1.0, base=0,
                               pattern=[[-1, P]], channel_multiplier=1).then_inc(constants_set, 1)

            def hold(semaphore, value):
                pool.wait_ge(semaphore, value)
                pool.sem_inc(pool_turn, 1)

            def normalise(b, variance_at):
                pool.wait_ge(bank_free, variance_at)
                pool.tensor_tensor(rstd[:, :], variance[:, :], minus_half[:, :], ALU.pow).then_inc(rstd_ready, 1)
                pool.wait_ge(rstd_ready, b + 1)
                pool.tensor_tensor(gain[:, :], vec[:, GAMMA:GAMMA + CC], rstd[:, 0:1].broadcast_to([P, CC]),
                                   ALU.mult).then_inc(gain_ready, 1)
                hold(gain_ready, b + 1)
                for c in range(CC):
                    pool.tensor_scalar(x_in[:, c, :], x_in[:, c, :], neg_mean[:, 0:1], gain[:, c:c + 1],
                                       ALU.add, ALU.mult).then_inc(normalised, 1)

            def scale_rows(unit):
                for t in range(LAST):
                    hold(scale_ready, TILES * unit + t + 1)
                    pool.tensor_scalar(probs[:, t, :], probs[:, t, :], row_scale[:, t:t + 1], 1.0,
                                       ALU.mult, ALU.mult).then_inc(probs_ready, 1)

            pool.wait_ge(constants_set, 3)
            pool.wait_ge(vec_loaded, 16)
            normalise(0, 2)
            for i in POOL_PIECES:
                pool.wait_ge(weight_hi, hi_written(i))
                pool.tensor_tensor(pieces[i][1], staged[i], pieces[i][0].bitcast(F32),
                                   ALU.subtract).then_inc(weight_split_pool, 1)
            scale_rows(0)

            def batch(b, last):
                n = Tally()
                for u in range(UNITS):
                    for step in results(u, last):
                        n.add(step)
                        if step[0] == "variance":
                            variance_at = START.bank + BATCH.bank * b + n.bank
                    if u == 5 and not last:
                        normalise(b + 1, variance_at)
                    if u < UNITS - 1 or not last:
                        scale_rows(UNITS * b + u + 1)

            with pool.Fori(0, BATCHES - 1) as b:
                batch(b, False)
            batch(BATCHES - 1, True)

        @block.scalar
        def _(act):
            act.dma_start(vec[:, :], vectors).then_inc(vec_loaded, 16)

            def weights(i):
                act.wait_ge(stage_loaded[i], 16)
                hi = pieces[i][0]
                if i == HEADS:
                    act.activation(hi, staged[i], ACT.Copy).then_inc(weight_hi, 1)
                    return
                act.activation(staged[i][:, 0:QUERY], staged[i][:, 0:QUERY], ACT.Copy,
                               scale=SCALE).then_inc(weight_scaled, 1)
                act.activation(hi[:, QUERY:PIECE], staged[i][:, QUERY:PIECE], ACT.Copy).then_inc(weight_hi, 1)
                act.wait_ge(weight_scaled, i + 1)
                act.activation(hi[:, 0:QUERY], staged[i][:, 0:QUERY], ACT.Copy).then_inc(weight_hi, 1)

            def y_parts(b):
                for c in range(CC):
                    act.wait_ge(normalised, CC * b + c + 1)
                    act.activation(y_hi[:, c, :], x_in[:, c, :], ACT.Identity,
                                   bias=vec[:, BETA + c:BETA + c + 1]).then_inc(y_hi_ready, 1)

            def hi_part(step, b, n):
                if in_ring(step):
                    act.wait_ge(ring_ready, START.ring + BATCH.ring * b + n.ring + 1)
                    done = ring_hi
                else:
                    act.wait_ge(bank_ready, START.bank + BATCH.bank * b + n.bank + 1)
                    done = bank_hi
                if step[0] in ("q", "k"):
                    act.activation(pair_of(step)[0], psum(step, n), ACT.Identity, bias=bias(step)).then_inc(done, 1)
                else:
                    act.activation(pair_of(step)[0], psum(step, n), ACT.Copy).then_inc(done, 1)

            def psum(step, n):
                n.ring += START.ring
                where = psum_of(step, n)
                n.ring -= START.ring
                return where

            def exponentials(unit, turned=None):
                for t in range(TILES):
                    if turned is not None and t == 0:
                        act.wait_ge(ring_ready, turned)
                    act.wait_ge(max_ready, TILES * unit + t + 1)
                    s = 2 * (t % 2)
                    act.activation(probs[:, t, :], bank[:, s:s + 2, :].rearrange("p b n -> p (b n)"), ACT.Exp,
                                   bias=neg_max[:, t:t + 1], accum_out=row_sum[:, t:t + 1]).then_inc(exp_ready, 1)

            weights(0)
            weights(1)
            y_parts(0)
            for i in range(2, HEADS + 1):
                weights(i)
            act.wait_ge(q_bias_scaled, 1)
            before = Tally()
            for step in HEAD_START:
                if split_in_two(step):
                    if in_ring(step):
                        act.wait_ge(ring_ready, before.ring + 1)
                    else:
                        act.wait_ge(bank_ready, before.bank + 1)
                    act.activation(pair_of(step)[0], psum_of(step, before), ACT.Identity,
                                   bias=bias(step)).then_inc(ring_hi if in_ring(step) else bank_hi, 1)
                before.add(step)
            act.wait_ge(weight_split_dve, len(DVE_PIECES))
            act.wait_ge(weight_split_pool, 1)
            exponentials(0)

            def batch(b, last):
                n = Tally()
                for u in range(UNITS):
                    h, half = divmod(u, 2)
                    if u == UNITS - 1 and not last:
                        y_parts(b + 1)
                    for step in results(u, last):
                        if step[0] == "turned" and step[2] >= HI_SLOTS:
                            act.wait_ge(attend_done, KEYS * (UNITS * b + u) + step[2] - HI_SLOTS + 1)
                        if split_in_two(step):
                            hi_part(step, b, n)
                        n.add(step)
                    act.wait_ge(attend_done, KEYS * (UNITS * b + u + 1))
                    act.activation(o_hi[:, h, half * HALF:(half + 1) * HALF], attended[:, :],
                                   ACT.Copy).then_inc(o_hi_ready, 1)
                    if u < UNITS - 1 or not last:
                        exponentials(UNITS * b + u + 1, START.ring + BATCH.ring * b + n.ring)

            with act.Fori(0, BATCHES - 1) as b:
                batch(b, False)
            batch(BATCHES - 1, True)

        @block.vector
        def _(dve):
            def weights(i):
                dve.wait_ge(weight_hi, hi_written(i))
                dve.tensor_tensor(pieces[i][1], staged[i], pieces[i][0].bitcast(F32),
                                  ALU.subtract).then_inc(weight_split_dve, 1)

            def partition_statistics(b):
                for c in range(CC):
                    dve.wait_ge(x_loaded[c], 16 * b + 16)
                    for half in range(2):
                        dve.bn_stats(bn[:, 2 * c + half, :],
                                     x_in[:, c, half * HALF:(half + 1) * HALF]).then_inc(bn_done, 1)
                dve.wait_ge(bn_done, 2 * CC * (b + 1))
                dve.sem_inc(dve_turn, 1)
                dve.bn_aggr(part[:, :], bn[:, :, :].rearrange("p a s -> p (a s)")).then_inc(part_ready, 1)

            def whole_mean(b, psum, ready_at):
                dve.wait_ge(bank_ready, ready_at)
                dve.tensor_scalar(neg_mean[:, :], psum[:, 0:1], -1.0, None, ALU.mult).then_inc(bank_free, 1)
                dve.wait_ge(bank_free, ready_at)
                dve.tensor_tensor(offset[:, :], part[:, 0:1], neg_mean[:, :], ALU.add).then_inc(offset_ready, 1)
                dve.wait_ge(offset_ready, b + 1)
                dve.scalar_tensor_tensor(spread[:, :], offset[:, :], offset[:, 0:1], part[:, 1:2], ALU.mult,
                                         ALU.add).then_inc(spread_ready, 1)

            def whole_variance(psum, ready_at):
                dve.wait_ge(bank_ready, ready_at)
                dve.tensor_scalar(variance[:, :], psum[:, 0:1], EPS, None, ALU.add).then_inc(bank_free, 1)

            def y_parts(b):
                for c in range(CC):
                    dve.wait_ge(y_hi_ready, CC * b + c + 1)
                    dve.scalar_tensor_tensor(y_lo[:, c, :], x_in[:, c, :], vec[:, BETA + c:BETA + c + 1],
                                             y_hi[:, c, :].bitcast(F32), ALU.add, ALU.subtract).then_inc(y_ready, 1)

            def softmax(unit, first_result=lambda: None, while_filling=lambda: None):
                def maximum(t):
                    dve.wait_ge(scores_ready, TILES * unit + t + 1)
                    s = 2 * (t % 2)
                    dve.tensor_reduce(neg_max[:, t:t + 1], bank[:, s:s + 2, :].rearrange("p b n -> p (b n)"),
                                      AX_X, ALU.max, negate=True).then_inc(max_ready, 1)

                def inverse(t):
                    dve.wait_ge(exp_ready, TILES * unit + t + 1)
                    dve.reciprocal(row_scale[:, t:t + 1], row_sum[:, t:t + 1]).then_inc(scale_ready, 1)

                for t in range(TILES):
                    maximum(t)
                    if t == 1:
                        inverse(0)
                        while_filling()
                        inverse(1)
                inverse(2)
                first_result()
                inverse(LAST)
                dve.wait_ge(scale_ready, TILES * (unit + 1))
                for a, z in ((0, FIRST), (FIRST, S)):
                    dve.tensor_scalar(probs[:, LAST, a:z], probs[:, LAST, a:z], row_scale[:, LAST:TILES], None,
                                      ALU.mult).then_inc(last_probs_ready, 1)

            def finish(step, b, n, start=START):
                kind, h, m = step
                ring_at = start.ring + BATCH.ring * b + n.ring + 1
                bank_at = start.bank + BATCH.bank * b + n.bank + 1
                at_start = Tally()
                at_start.ring = start.ring + n.ring
                psum = psum_of(step, at_start)
                free = ring_free if in_ring(step) else bank_free
                if kind == "mean":
                    whole_mean(b + (start is START), psum, bank_at)
                elif kind == "variance":
                    whole_variance(psum, bank_at)
                elif split_in_two(step):
                    hi, lo = pair_of(step)
                    if in_ring(step):
                        dve.wait_ge(ring_hi, start.ring_hi + BATCH.ring_hi * b + n.ring_hi + 1)
                    else:
                        dve.wait_ge(bank_hi, start.bank_hi + BATCH.bank_hi * b + n.bank_hi + 1)
                    if kind in ("q", "k"):
                        dve.scalar_tensor_tensor(lo, psum, bias(step), hi.bitcast(F32), ALU.add,
                                                 ALU.subtract).then_inc(free, 1)
                    else:
                        dve.tensor_tensor(lo, psum, hi.bitcast(F32), ALU.subtract).then_inc(free, 1)
                elif kind == "vt":
                    dve.wait_ge(ring_ready, ring_at)
                    dve.tensor_scalar(vt[:, m * HALF:(m + 1) * HALF], psum, bias(step), None,
                                      ALU.add).then_inc(free, 1)
                else:
                    if in_ring(step):
                        dve.wait_ge(ring_ready, ring_at)
                    else:
                        dve.wait_ge(bank_ready, bank_at)
                    dve.wait_ge(rows_loaded[m], 32 * b + 16 * h + 16)
                    dve.scalar_tensor_tensor(rows[:, m, :], psum, bias(step), rows[:, m, :], ALU.add,
                                             ALU.add).then_inc(rows_ready, 1)
                    dve.wait_ge(rows_ready, 2 * CC * b + CC * h + m + 1)
                    dve.sem_inc(free, 1)

            dve.wait_ge(vec_loaded, 16)
            dve.tensor_scalar(vec[:, QKV_B:QKV_B + HEADS], vec[:, QKV_B:QKV_B + HEADS], SCALE, None,
                              ALU.mult).then_inc(q_bias_scaled, 1)
            dve.memset(offset[:, :], 0.0).then_inc(attended_free, 1)
            partition_statistics(0)
            before = Tally()

            def take_first(step):
                finish(step, 0, before, Tally())
                before.add(step)

            for step in HEAD_START[:2]:
                take_first(step)
            weights(0)
            weights(1)
            y_parts(0)
            weights(2)
            for step in HEAD_START[2:-1]:
                take_first(step)
            softmax(0, while_filling=lambda: take_first(HEAD_START[-1]))

            def batch(b, last):
                n = Tally()

                def take(step):
                    finish(step, b, n)
                    n.add(step)

                for u in range(UNITS):
                    h, half = divmod(u, 2)
                    if u == 3 and not last:
                        partition_statistics(b + 1)
                    if u == UNITS - 1 and not last:
                        y_parts(b + 1)
                    for step in results(u, last)[1 if u > 0 else 0:]:
                        if step[0] == "turned" and step[2] >= RING:
                            dve.wait_ge(attend_done, KEYS * (UNITS * b + u) + step[2] - RING + 1)
                        take(step)
                    dve.wait_ge(o_hi_ready, UNITS * b + u + 1)
                    at = slice(half * HALF, (half + 1) * HALF)
                    dve.tensor_tensor(o_lo[:, h, at], attended[:, :], o_hi[:, h, at].bitcast(F32),
                                      ALU.subtract).then_inc(attended_free, 1)
                    first = results(u + 1, last)[0] if u < UNITS - 1 else TAIL[0]
                    if u < UNITS - 1 or not last:
                        softmax(UNITS * b + u + 1, lambda: take(first))
                for step in TAIL[0 if last else 1:]:
                    take(step)

            with dve.Fori(0, BATCHES - 1) as b:
                batch(b, False)
            batch(BATCHES - 1, True)

        @block.tensor
        def _(pe):
            def product(psum, a, z, stationary, moving, contractions, begin=0, end=None):
                last = PASSES * contractions - 1
                for m in range(begin, last + 1 if end is None else end):
                    i, which = divmod(m, PASSES)
                    s_hi, s_lo = stationary(i)
                    m_hi, m_lo = moving(i)
                    left, right = ((s_hi, m_hi), (s_hi, m_lo), (s_lo, m_hi))[which]
                    done = nc.tensor.matmul(psum[:, a:z], left, right, start=(m == 0), stop=(m == last))
                return done

            def project_y(psum, h, which, half, begin=0, end=None):
                at = slice(half * HALF, (half + 1) * HALF)
                return product(psum, 0, HALF, lambda c: (w_hi[:, h, which, c, :], w_lo[:, h, which, c, :]),
                               lambda c: (y_hi[:, c, at], y_lo[:, c, at]), CC, begin, end)

            def run(step, psum, begin=0, end=CC * PASSES):
                kind, h, n = step
                if kind == "q":
                    return project_y(psum, h, Q, n, begin, end)
                if kind == "vt":
                    return project_y(psum, h, V, n, begin, end)
                if kind == "k":
                    project_y(bank[:, 0, :], h, K, 0, begin, end)
                    return project_y(bank[:, 1, :], h, K, 1, begin, end)
                if kind == "turn_v":
                    for i in range(KEYS // 2):
                        c = n * (KEYS // 2) + i
                        done = nc.tensor.transpose(psum[:, i * P:(i + 1) * P], vt[:, c * P:(c + 1) * P], ident[:, :])
                    return done
                if kind == "mean":
                    return nc.tensor.matmul(psum[:, 0:1], average[:, :], part[:, 0:1], start=True, stop=True)
                if kind == "variance":
                    return nc.tensor.matmul(psum[:, 0:1], average[:, :], spread[:, :], start=True, stop=True)
                at = slice(h * HALF, (h + 1) * HALF)
                return product(psum, 0, HALF,
                               lambda c: (wo_hi[:, c, n * P:(n + 1) * P], wo_lo[:, c, n * P:(n + 1) * P]),
                               lambda c: (o_hi[:, c, at], o_lo[:, c, at]), CC, begin, end)

            def score_tile(t):
                s = 2 * (t % 2)
                tile = slice(t * P, (t + 1) * P)
                for half in range(2):
                    at = slice(half * HALF, (half + 1) * HALF)
                    done = product(bank[:, s + half, :], 0, HALF, lambda i: (q_hi[:, tile], q_lo[:, tile]),
                                   lambda i: (k_hi[:, at], k_lo[:, at]), 1)
                return done

            def scores(free_at, unit, begin_fill=lambda: None):
                pe.wait_ge(bank_free, free_at)
                for t in range(TILES):
                    if t == 2:
                        begin_fill()
                    if t >= 2:
                        pe.wait_ge(exp_ready, TILES * unit + t - 1)
                    score_tile(t).then_inc(scores_ready, 1)

            pe.wait_ge(constants_set, 3)
            before = Tally()
            for step in HEAD_START[:-1]:
                begin = 0
                if step[0] == "mean":
                    pe.wait_ge(part_ready, 1)
                elif step[0] == "variance":
                    pe.wait_ge(spread_ready, 1)
                elif step[0] == "k":
                    pe.wait_ge(weight_split_dve, 1)
                    for c in range(CC - 1):
                        pe.wait_ge(y_ready, c + 1)
                        run(step, psum_of(step, before), PASSES * c, PASSES * (c + 1))
                    pe.wait_ge(y_ready, CC)
                    begin = PASSES * (CC - 1)
                run(step, psum_of(step, before), begin).then_inc(ring_ready if in_ring(step) else bank_ready, 1)
                before.add(step)
            step = HEAD_START[-1]
            cut_at = (CC - 1) * PASSES
            run(step, psum_of(step, before), 0, cut_at)
            pe.wait_ge(ring_free, before.ring)
            scores(START.bank, 0, lambda: run(step, psum_of(step, before), cut_at).then_inc(ring_ready, 1))
            pe.wait_ge(weight_split_dve, len(DVE_PIECES))
            pe.wait_ge(weight_split_pool, len(POOL_PIECES) - 1)

            def batch(b, last):
                n = Tally()

                def ring_bank():
                    pe.wait_ge(ring_free, BATCH.ring * b + START.ring + max(n.ring + 1 - RING, 0))
                    return ring[:, (START.ring + n.ring) % RING, :]

                def fill(step, unit, begin=0, end=CC * PASSES):
                    kind, h, m = step
                    if begin == 0:
                        if in_ring(step):
                            ring_bank()
                        elif min(score_banks(step)) < 2:
                            pe.wait_ge(exp_ready, TILES * unit + TILES - 1)
                        else:
                            pe.wait_ge(exp_ready, TILES * unit + TILES)
                        if h == 0 and (kind == "k" or (kind == "q" and m == 1)):
                            pe.wait_ge(bank_free, START.bank + BATCH.bank * b + n.bank)
                        if kind == "turn_v" and m == 1:
                            pe.wait_ge(ring_free, START.ring + BATCH.ring * b + n.ring - 1)
                        if kind == "vt" and h == 0 and m == 0:
                            pe.wait_ge(y_ready, CC * (b + 2))
                        if kind == "mean":
                            pe.wait_ge(part_ready, b + 2)
                        if kind == "variance":
                            pe.wait_ge(spread_ready, b + 2)
                        if kind == "project" and m == 0 and not isinstance(b, int):
                            pe.wait_ge(weight_split_pool, len(POOL_PIECES))
                    if kind == "project" and m == 0 and begin == (NO_LAST_HEAD if last and h == 1 else 0):
                        pe.wait_ge(attended_free, UNITS * b + (UNITS if h == 0 else UNITS + 1))
                    at_start = Tally()
                    at_start.ring = START.ring + n.ring
                    done = run(step, psum_of(step, at_start), begin, end)
                    if end == CC * PASSES:
                        done.then_inc(ring_ready if in_ring(step) else bank_ready, 1)
                        n.add(step)

                def turn(c):
                    where = ring_bank()
                    if c == FIRST // P:
                        pe.wait_ge(last_probs_ready, 2 * unit + 2)
                    for t in range(TILES):
                        done = nc.tensor.transpose(where[:, t * P:(t + 1) * P], probs[:, t, c * P:(c + 1) * P],
                                                   ident[:, :])
                    done.then_inc(ring_ready, 1)
                    n.add(("turned", 0, c))

                def turn_first(unit):
                    wheres, counts = [], []
                    for c in range(2):
                        wheres.append(ring_bank())
                        n.add(("turned", 0, c))
                        counts.append(START.ring + BATCH.ring * b + n.ring)
                    pe.wait_ge(probs_ready, LAST * (unit + 1))
                    for t in range(TILES):
                        if t == LAST:
                            pe.wait_ge(last_probs_ready, 2 * unit + 1)
                        for c in range(2):
                            done = nc.tensor.transpose(wheres[c][:, t * P:(t + 1) * P],
                                                       probs[:, t, c * P:(c + 1) * P], ident[:, :])
                            if t == LAST:
                                done.then_inc(ring_ready, 1)
                    return counts

                def attend(c, turned_at):
                    pe.wait_ge(ring_free, turned_at)
                    product(attended, 0, HALF, lambda i: (v_hi[:, i, :], v_lo[:, i, :]),
                            lambda i: (turned_hi[:, i % HI_SLOTS, :], turned_lo[:, i % RING, :]), KEYS, PASSES * c,
                            PASSES * (c + 1)).then_inc(attend_done, 1)

                for u in range(UNITS):
                    unit = UNITS * b + u
                    before, slipped, beside, after = fills(u, last)
                    for i, step in enumerate(before):
                        fill(step, unit, CUT if i == 0 and u > 0 else 0)
                    fill(slipped, unit, 0, CC * PASSES - slip(slipped))
                    for step in beside:
                        fill(step, unit)
                        v_at = START.bank + BATCH.bank * b + n.bank
                    turned_at = turn_first(unit)

                    def turn_next():
                        turn(len(turned_at))
                        turned_at.append(START.ring + BATCH.ring * b + n.ring)

                    fill(slipped, unit, CC * PASSES - slip(slipped))
                    for step in after:
                        fill(step, unit)
                    turn_next()
                    pe.wait_ge(attended_free, unit + 1)
                    for c in range(KEYS):
                        if len(turned_at) < KEYS:
                            turn_next()
                        if c == KEYS // 2 and u % 2 == 0:
                            pe.wait_ge(bank_free, v_at)
                        attend(c, turned_at[c])
                    if u < UNITS - 1:
                        first = fills(u + 1, last)[0][0]
                    else:
                        first = TAIL[0]
                    if u < UNITS - 1 or not last:
                        scores(START.bank + BATCH.bank * b + n.bank, unit + 1,
                               lambda: fill(first, unit + 1, 0, CUT))
                if last:
                    fill(TAIL[0], UNITS * b + UNITS - 1, 0, NO_LAST_HEAD)
                for i, step in enumerate(TAIL):
                    fill(step, UNITS * b + (UNITS - 1 if last else UNITS),
                         0 if i > 0 else NO_LAST_HEAD if last else CUT)

            with pe.Fori(0, BATCHES - 1) as b:
                batch(b, False)
            batch(BATCHES - 1, True)


def kernel(x, L0_conv_gn_weight, L0_conv_gn_bias, L0_conv_qkv_w, L0_conv_qkv_b, L0_conv_out_w, L0_conv_out_b):
    import numpy as np
    from concourse import bacc
    from concourse.bass_utils import run_bass_kernel_spmd

    def columns(v):
        return np.asarray(v).reshape(-1, P).T

    x = np.asarray(x)
    arrays = {
        "x_dram": np.ascontiguousarray(x.reshape(BATCHES, C, S)),
        "w_qkv_dram": np.ascontiguousarray(
            np.asarray(L0_conv_qkv_w).reshape(3, HEADS, D, CC, P).transpose(4, 1, 0, 3, 2).reshape(P, HEADS, 3 * CC * D)),
        "w_out_dram": np.ascontiguousarray(
            np.asarray(L0_conv_out_w).reshape(C, HEADS, D).transpose(2, 1, 0).reshape(P, HEADS * C)),
        "vectors_dram": np.ascontiguousarray(np.concatenate(
            [columns(L0_conv_gn_weight), columns(L0_conv_gn_bias), columns(L0_conv_qkv_b), columns(L0_conv_out_b)], axis=1)),
    }
    nc = bacc.Bacc("TRN2", target_bir_lowering=False, num_devices=1)
    args = [nc.dram_tensor(name, a.shape, F32, kind="ExternalInput").ap() for name, a in arrays.items()]
    out = nc.dram_tensor("out_dram", (BATCHES, C, S), F32, kind="ExternalOutput").ap()
    attention_program(nc, *args, out)
    r = run_bass_kernel_spmd(nc, [arrays], core_ids=[0])
    return r.results[0]["out_dram"].reshape(x.shape)
```
